# Optimizing a Trainium2 kernel written in Bass

```python
import numpy as np
import jax
import jax.numpy as jnp

def _softmax(x, axis=-1):
    return jax.nn.softmax(x, axis=axis)

def _gelu(x):
    return jax.nn.gelu(x, approximate=True)

def _silu(x):
    return jax.nn.silu(x)

def _sigmoid(x):
    return jax.nn.sigmoid(x)

def _layernorm(x, axis=-1, eps=1e-05):
    m = jnp.mean(x, axis=axis, keepdims=True)
    v = jnp.var(x, axis=axis, keepdims=True)
    return (x - m) / jnp.sqrt(v + eps)

def _scatter_add(tgt, idx, src, axis=0):
    return tgt.at[idx].add(src)

def _segment_sum(src, seg, n):
    return jax.ops.segment_sum(src, seg, n)
kernel_name = 'mk_seq_preln_d1_jaxref_r4_d5dede'

def setup_inputs(seed: int=0):
    np.random.seed(seed)
    _w = jnp.asarray

    def _L0_attn_setup():
        import math
        import jax, jax.numpy as jnp
        import numpy as np
        D_MODEL = 256
        N_HEADS = 16
        HEAD_DIM = D_MODEL // N_HEADS
        B, L = (1, 1024)

        def _slopes(n_heads):
            ratio = 2.0 ** (-8.0 / n_heads)
            return jnp.asarray([ratio ** (i + 1) for i in range(n_heads)], dtype=jnp.float32)
        key = jax.random.key(seed)
        ks = jax.random.split(key, 5)
        scale = 1.0 / math.sqrt(D_MODEL)
        return {'x': jax.random.normal(ks[0], (B, L, D_MODEL), dtype=jnp.float32), 'q_w': jax.random.normal(ks[1], (D_MODEL, D_MODEL), dtype=jnp.float32) * scale, 'k_w': jax.random.normal(ks[2], (D_MODEL, D_MODEL), dtype=jnp.float32) * scale, 'v_w': jax.random.normal(ks[3], (D_MODEL, D_MODEL), dtype=jnp.float32) * scale, 'o_w': jax.random.normal(ks[4], (D_MODEL, D_MODEL), dtype=jnp.float32) * scale}
    _L0_attn_in = _L0_attn_setup()

    def _L0_ffn_setup():
        import jax, jax.numpy as jnp
        import numpy as np
        B, S, D, F, E = (8, 256, 256, 1024, 8)
        EPS = 1e-05
        key = jax.random.key(seed)
        ks = jax.random.split(key, 4)
        s = 0.02
        return {'input_features': jax.random.normal(ks[0], (B, S, D), jnp.float32), 'centroids': jax.random.normal(ks[1], (E, D), jnp.float32) * 0.1, 'ln_g': jnp.ones((E, D), jnp.float32), 'ln_b': jnp.zeros((E, D), jnp.float32), 'w1': jax.random.normal(ks[2], (E, D, F), jnp.float32) * s, 'b1': jnp.zeros((E, F), jnp.float32), 'w2': jax.random.normal(ks[3], (E, F, D), jnp.float32) * s, 'b2': jnp.zeros((E, D), jnp.float32)}
    _L0_ffn_in = _L0_ffn_setup()
    _d = {'L0_attn_x': _L0_attn_in['x'], 'L0_attn_q_w': _L0_attn_in['q_w'], 'L0_attn_k_w': _L0_attn_in['k_w'], 'L0_attn_v_w': _L0_attn_in['v_w'], 'L0_attn_o_w': _L0_attn_in['o_w'], 'L0_ffn_centroids': _L0_ffn_in['centroids'], 'L0_ffn_ln_g': _L0_ffn_in['ln_g'], 'L0_ffn_ln_b': _L0_ffn_in['ln_b'], 'L0_ffn_w1': _L0_ffn_in['w1'], 'L0_ffn_b1': _L0_ffn_in['b1'], 'L0_ffn_w2': _L0_ffn_in['w2'], 'L0_ffn_b2': _L0_ffn_in['b2']}
    _x0 = _d['L0_attn_x']
    _d['L0_attn_x'] = jax.random.normal(jax.random.fold_in(jax.random.key(seed), 1), (4, 1024, 256), dtype=_x0.dtype)
    del _x0
    return _d

def reference(L0_attn_x, L0_attn_q_w, L0_attn_k_w, L0_attn_v_w, L0_attn_o_w, L0_ffn_centroids, L0_ffn_ln_g, L0_ffn_ln_b, L0_ffn_w1, L0_ffn_b1, L0_ffn_w2, L0_ffn_b2):

    def _L0_attn_ref(x, q_w, k_w, v_w, o_w):
        import math
        import jax, jax.numpy as jnp
        import numpy as np
        D_MODEL = 256
        N_HEADS = 16
        HEAD_DIM = D_MODEL // N_HEADS
        B, L = (1, 1024)

        def _slopes(n_heads):
            ratio = 2.0 ** (-8.0 / n_heads)
            return jnp.asarray([ratio ** (i + 1) for i in range(n_heads)], dtype=jnp.float32)
        b, l, _ = x.shape

        def proj(w):
            return (x @ w).reshape(b, l, N_HEADS, HEAD_DIM).transpose(0, 2, 1, 3)
        q, k, v = (proj(q_w), proj(k_w), proj(v_w))
        scale = math.sqrt(HEAD_DIM)
        scores = jnp.einsum('bhid,bhjd->bhij', q, k) / scale
        pos = jnp.arange(l)
        distance = jnp.abs(pos[None, :] - pos[:, None]).astype(jnp.float32)
        alibi = -distance[None, :, :] * _slopes(N_HEADS)[:, None, None]
        scores = scores + alibi[None]
        causal = pos[None, :] <= pos[:, None]
        scores = jnp.where(causal[None, None], scores, -jnp.inf)
        attn = jax.nn.softmax(scores, axis=-1)
        out = jnp.einsum('bhij,bhjd->bhid', attn, v)
        out = out.transpose(0, 2, 1, 3).reshape(b, l, D_MODEL)
        return out @ o_w

    def _L0_ffn_ref(input_features, centroids, ln_g, ln_b, w1, b1, w2, b2):
        import jax, jax.numpy as jnp
        import numpy as np
        B, S, D, F, E = (8, 256, 256, 1024, 8)
        EPS = 1e-05
        x = input_features.reshape(-1, D)
        aff = jax.lax.stop_gradient(x @ centroids.T)
        eid = jnp.argmax(aff, axis=-1)
        alpha = jax.nn.sigmoid(jnp.sum(x * centroids[eid], axis=-1, keepdims=True))
        mu = jnp.mean(x, axis=-1, keepdims=True)
        var = jnp.mean((x - mu) ** 2, axis=-1, keepdims=True)
        xn = (x - mu) * jax.lax.rsqrt(var + EPS)
        xln = xn * ln_g[eid] + ln_b[eid]
        onehot = jax.nn.one_hot(eid, E, dtype=x.dtype)
        ffn = jnp.zeros_like(x)
        for e in range(E):
            h = jax.nn.relu(xln @ w1[e] + b1[e])
            ffn = ffn + onehot[:, e:e + 1] * (h @ w2[e] + b2[e])
        out = x + alpha * ffn
        return out.reshape(input_features.shape)
    x = L0_attn_x
    x = x + _L0_attn_ref(_layernorm(x, axis=-1), L0_attn_q_w, L0_attn_k_w, L0_attn_v_w, L0_attn_o_w)
    x = x + _L0_ffn_ref(_layernorm(x, axis=-1), L0_ffn_centroids, L0_ffn_ln_g, L0_ffn_ln_b, L0_ffn_w1, L0_ffn_b1, L0_ffn_w2, L0_ffn_b2)
    return x

_drawn_inputs = setup_inputs


def setup_inputs(seed=0):
    import zlib

    import numpy as np

    out = dict(_drawn_inputs(seed))
    spreads = {'L0_ffn_ln_g': (1.0, 0.6),
     'L0_ffn_ln_b': (0.0, 0.8),
     'L0_ffn_b1': (0.0, 0.41),
     'L0_ffn_b2': (0.0, 0.1)}
    factors = {}
    for name, (base, spread) in spreads.items():
        noise = np.random.default_rng([zlib.crc32(name.encode()), seed]).standard_normal(out[name].shape)
        drawn = base * np.exp(spread * noise) if base else spread * noise
        out[name] = jnp.asarray(drawn.astype(out[name].dtype))
    for name, factor in factors.items():
        out[name] = (out[name] * factor).astype(out[name].dtype)
    return out
```

```python
from contextlib import ExitStack

import concourse.bass as bass
from concourse import mybir


P = 128
B, L, D = 4, 1024, 256
H, HD = 16, 16
G = 4
HG = H // G
NG = B * G
KT = L // P
HALF = L // 2
F, E = 1024, 8
DC, FC = D // P, F // P
TOK = B * L
T = TOK // P
CH = TOK // HALF
TC = HALF // P
TILES = T + E - 1
LIST = TOK
LISTS = E * LIST + E * P
NO_TOKEN = 1 << 20
PK = 2 * D + 1
EPS = 1e-5
TABS = E * (FC + 3 * DC)
LOW = -3.0e38
UNROLL = 3
KS, KE = 99, 102
QPART = (0, 0, 0, 1, 1, 2)
KPART = (0, 1, 2, 0, 1, 0)

ALU = mybir.AluOpType
ACT = mybir.ActivationFunctionType
F32, BF16, I32 = mybir.dt.float32, mybir.dt.bfloat16, mybir.dt.int32
AX = mybir.AxisListType.X

STEPS = [(0, k) for k in range(4)] + [(1, k) for k in range(8)]
NS = len(STEPS)
CHUNKS = [(3, 0), (2, 0), (1, 0), (0, 0),
          (7, 0), (7, 1), (6, 0), (5, 0), (4, 0), (6, 1), (5, 1), (4, 1)]


def first_col(s):
    half, kt = STEPS[s]
    return max(kt * P - half * HALF, 0)


def chunk_cols(s):
    t, c = CHUNKS[s]
    return min(HALF, (t + 1) * P - c * HALF)


def on_diagonal(s):
    half, kt = STEPS[s]
    return kt // 4 == half


DIAG = [s for s in range(NS) if on_diagonal(s)]


def layer_kernel(nc, x, wq, wk, wv, wo, cent, ln_g, ln_b, w1, b1, w2, b2,
                 ident, identh, before, later, mask, alibi, tokens, consts, out):
    ctx = ExitStack()

    def sb(name, shape, dt):
        return ctx.enter_context(nc.sbuf_tensor(name, shape, dt))

    def sem(name):
        return ctx.enter_context(nc.semaphore(name))

    with ctx:
        qk_dram = nc.dram_tensor("qk_parts", [2, 3, B * D, L], BF16).ap()
        pk_dram = nc.dram_tensor("packed_tokens", [TOK, PK], F32).ap()
        list_dram = nc.dram_tensor("expert_lists", [LISTS, 1], I32).ap()

        identF = sb("identF", [P, P], F32)
        identB = sb("identB", [P, P], BF16)
        beforeB = sb("beforeB", [P, P], BF16)
        laterB = sb("laterB", [P, P], BF16)
        onesB = sb("onesB", [P, P], BF16)
        maskF = sb("maskF", [P, HALF], F32)
        wqkv = sb("wqkv", [P, 3, DC, D], F32)
        wos = sb("wos", [P, DC, D], F32)
        tok_id = sb("tok_id", [P, T], I32)
        cst = sb("cst", [P, 96], F32)
        no_tok = sb("no_tok", [P, LISTS // P], I32)
        tabs = sb("tabs", [P, P], F32)
        tabT = sb("tabT", [P, TABS], F32)
        b2r = sb("b2r", [P, E * D], F32)
        neg_half = sb("neg_half", [P, TC], F32)
        mx = sb("mx", [P, 4, HG, TC], F32)
        nm = sb("nm", [P, 2, HG * TC], F32)
        mparts = sb("mparts", [P, 3, HG * TC], BF16)
        mrows = sb("mrows", [3 * HG * TC, 2, P], BF16)
        cum = sb("cum", [P, 2, E], F32)
        cumB = sb("cumB", [P, 2, E], BF16)
        rt = sb("rt", [P, 4, TC, E], F32)
        rs = sb("rs", [P, 4, TC], F32)
        csum = sb("csum", [P, E], F32)
        ohB = sb("ohB", [P, 2, TC, E], BF16)
        slot = sb("slot", [P, 2, TC], I32)
        slot_tok = sb("slot_tok", [P, 2, TC], I32)
        tcmp = sb("tcmp", [P, 40 * 8], F32)
        tt = sb("tt", [P, 8, 40], F32)
        tile_tab = sb("tile_tab", [P, 2, 40], I32)
        st6 = sb("st6", [P, 2, TC, 6], F32)
        mv = sb("mv", [P, 2, TC, 2], F32)
        var = sb("var", [P, 2, TC], F32)
        rstd = sb("rstd", [P, 2, TC], F32)
        ids_g = [sb(f"ids_g{u}", [P, 1], I32) for u in range(UNROLL)]
        ids_s = [sb(f"ids_s{u}", [P, 1], I32) for u in range(UNROLL)]
        alph = sb("alph", [P, UNROLL, 3], F32)

        ARENA = 43 * 1024
        arena = sb("arena", [P, ARENA], F32)

        def carve(at, shape, dt=F32):
            n = 1
            for d in shape:
                n *= d
            cols = n if dt == F32 else n // 2
            assert at + cols <= ARENA, (at, cols)
            v = arena[:, at:at + cols]
            if dt != F32:
                v = v.bitcast(dt)
            if len(shape) == 2:
                v = v.rearrange("p (a b) -> p a b", a=shape[0])
            elif len(shape) == 3:
                v = v.rearrange("p (a b c) -> p a b c", a=shape[0], b=shape[1])
            return v, at + cols

        va, p0 = carve(0, [NG * KT * 64])
        q_aug, k_aug, v_grp, probs = [], [], [], []
        for u in range(UNROLL):
            v, p0 = carve(p0, [2, HG, HALF], BF16)
            q_aug.append(v)
            v, p0 = carve(p0, [HG, L], BF16)
            k_aug.append(v)
        x_in, a0 = carve(p0, [2, TC, D])
        xn, a0 = carve(a0, [2, TC, D])
        xnT, a0 = carve(a0, [2, DC, HALF])
        p1 = p0
        for u in range(UNROLL):
            v, p1 = carve(p1, [HG, HALF])
            probs.append(v)
        assert a0 <= p1
        for u in range(UNROLL):
            v, p1 = carve(p1, [KT, HG, 32])
            v_grp.append(v)
        o_sb, p1 = carve(p1, [2, HALF])
        rec, p1 = carve(p1, [TC, HG])
        ao, a1 = carve(p1, [NG * KT * 64])
        parts, a0 = carve(p1, [2, 4, 3 * HALF], BF16)
        resid, a0 = carve(a0, [2, HALF])

        w1s, w2_at = carve(0, [E, DC * F])
        stage, c0 = carve(w2_at, [2, TC, D])
        aoT, c0 = carve(c0, [2, DC, HALF])
        xr, c0 = carve(c0, [2, TC, D])
        x1, c0 = carve(c0, [2, TC, D])
        ys, c0 = carve(c0, [2, TC, D])
        yT, c0 = carve(c0, [2, DC, HALF])
        assert c0 <= p1
        pks, c0 = carve(a1, [2, TC, PK])

        w2s, d0 = carve(w2_at, [E, FC * D])
        gat, d0 = carve(d0, [UNROLL, PK])
        eT, d0 = carve(d0, [UNROLL, DC, P])
        hs, d0 = carve(d0, [F])
        hT, d0 = carve(d0, [FC, P])
        yo, d0 = carve(d0, [UNROLL, 2 * D])

        ps = ctx.enter_context(nc.psum_tensor("ps", [P, 8, HALF], F32))

        CONSTS = 16
        const_in = sem("const_in")
        apart = sem("apart")
        fill = sem("fill")
        ones_s = sem("ones_s")
        pool_chain = sem("pool_chain")
        tab_ready, tab_sb = sem("tab_ready"), sem("tab_sb")
        lists_clear = sem("lists_clear")
        x_got = [sem(f"x_got{f}") for f in range(2)]
        stats = sem("stats")
        var_s = sem("var_s")
        rstd_s = sem("rstd_s")
        xn_s = sem("xn_s")
        xt_ready = sem("xt_ready")
        xt_sb = sem("xt_sb")
        qk_ready = sem("qk_ready")
        part1_s = sem("part1_s")
        resid_s = sem("resid_s")
        part2_s = sem("part2_s")
        part3_s = sem("part3_s")
        parts_out = [sem(f"parts_out{f}") for f in range(2)]
        v_ready = sem("v_ready")
        v_sb = sem("v_sb")
        aug_in = [sem(f"aug_in{u}") for u in range(UNROLL)]
        vg_s = sem("vg_s")
        s_ready = sem("s_ready")
        max_s = sem("max_s")
        comb_s = sem("comb_s")
        mneg_s = sem("mneg_s")
        mparts_s = sem("mparts_s")
        mt_ready = sem("mt_ready")
        mt_sb = sem("mt_sb")
        m_in = [sem(f"m_in{h}") for h in range(2)]
        st_ready = sem("st_ready")
        exp_s = sem("exp_s")
        pv_s = sem("pv_s")
        o_sb_s = sem("o_sb_s")
        ot_ready = sem("ot_ready")
        rec_s = sem("rec_s")
        ao_s = sem("ao_s")
        xr_in = [sem(f"xr_in{f}") for f in range(2)]
        w1_in, w2_in = sem("w1_in"), sem("w2_in")
        stage_s = sem("stage_s")
        at_ready, at_sb = sem("at_ready"), sem("at_sb")
        proj_ready = sem("proj_ready")
        x1_s = sem("x1_s")
        dve_chain = sem("dve_chain")
        y_s = sem("y_s")
        yn_s = sem("yn_s")
        z_s = sem("z_s")
        var_c, rstd_c = sem("var_c"), sem("rstd_c")
        stats_c = sem("stats_c")
        yt_ready, yt_sb = sem("yt_ready"), sem("yt_sb")
        aff_ready = sem("aff_ready")
        score_s = sem("score_s")
        oh_s = sem("oh_s")
        rank_ready = sem("rank_ready")
        slot_s = sem("slot_s")
        ids_out = [sem(f"ids_out{f}") for f in range(2)]
        pk_out = [sem(f"pk_out{f}") for f in range(2)]
        lists_done = sem("lists_done")
        packed_done = sem("packed_done")
        count_ready = sem("count_ready")
        table_s = sem("table_s")
        idg_in = [sem(f"idg_in{u}") for u in range(UNROLL)]
        ids_in = [sem(f"ids_in{u}") for u in range(UNROLL)]
        gat_in = [sem(f"gat_in{u}") for u in range(UNROLL)]
        et_ready, et_sb = sem("et_ready"), sem("et_sb")
        h_ready = sem("h_ready")
        h_act, h_dve = sem("h_act"), sem("h_dve")
        ht_ready = sem("ht_ready")
        ht_act, ht_dve = sem("ht_act"), sem("ht_dve")
        ye_ready = sem("ye_ready")
        alph_s = sem("alph_s")
        yo_s = sem("yo_s")
        y_chain = sem("y_chain")
        out_s = [sem(f"out_s{u}") for u in range(UNROLL)]

        x_rows = x.rearrange("b l d -> (b l) d")
        out_rows = out.rearrange("b l d -> (b l) d")
        pk_rows = pk_dram.rearrange("(j t p) c -> j p t c", t=TC, p=P)
        AUG_DMAS = 2 * len(QPART) + 1

        def after(eng, s, value):
            if not (isinstance(value, int) and value <= 0):
                eng.wait_ge(s, value)

        def wait_apart(eng, s, value):
            after(eng, s, value)
            if not isinstance(value, int):
                eng.sem_inc(apart, 1)

        def chunks_of(eng, body):
            body(0, 0, False)
            body(0, 1, False)
            with eng.Fori(1, B - 1) as b:
                body(b, 0, False)
                body(b, 1, False)
            body(B - 1, 0, False)
            body(B - 1, 1, True)

        def groups_of(eng, body):
            body(0, 0)
            with eng.Fori(0, 4) as it:
                for i in range(UNROLL):
                    body(it * UNROLL + (1 + i), (1 + i) % UNROLL, rounds=it + 2 if i == 2 else it + 1)
            for n in range(NG - 3, NG):
                body(n, n % UNROLL)

        def tiles_of(eng, body):
            for u in range(UNROLL):
                body(u, u, 0)
            with eng.Fori(1, TILES // UNROLL - 1) as it:
                for u in range(UNROLL):
                    body(it * UNROLL + u, u, it)
            for u in range(UNROLL):
                body(TILES - UNROLL + u, u, TILES // UNROLL - 1)

        block = ctx.enter_context(nc.Block())

        @block.sync
        def _(sp):
            def load_x(b, f):
                src = x_rows[bass.ds(b * L + f * HALF, HALF), :].rearrange("(t p) d -> p t d", p=P)
                sp.dma_start(x_in[:, f], src).then_inc(x_got[f], 16)

            load_x(0, 0)
            sp.dma_start(identF[:, :], ident).then_inc(const_in, 16)
            for i, w in enumerate((wq, wk, wv)):
                sp.dma_start(wqkv[:, i], w.rearrange("(c p) n -> p c n", p=P)).then_inc(const_in, 16)
            load_x(0, 1)
            sp.dma_start(wos[:, :, :], wo.rearrange("(c p) n -> p c n", p=P)).then_inc(const_in, 16)
            sp.dma_start(identB[:, :], identh).then_inc(const_in, 16)
            sp.dma_start(beforeB[:, :], before).then_inc(const_in, 16)
            sp.dma_start(laterB[:, :], later).then_inc(const_in, 16)
            sp.dma_start(maskF[:, :], mask).then_inc(const_in, 16)
            sp.dma_start(tok_id[:, :], tokens).then_inc(const_in, 16)
            sp.dma_start(cst[:, :], consts).then_inc(const_in, 16)
            for at, t in ((0, b1), (E * FC, ln_g), (E * (FC + DC), ln_b), (E * (FC + 2 * DC), cent)):
                rows = t.rearrange("e (c p) -> (e c) p", p=P)
                sp.dma_start(tabs[at:at + rows.shape[0], :], rows).then_inc(const_in, 16)
            b2row = b2.rearrange("(o e) d -> o (e d)", o=1)
            sp.dma_start(b2r[:, :], b2row.broadcast_to([P, E * D])).then_inc(const_in, 16)
            sp.wait_ge(fill, 1)
            sp.dma_start(list_dram.rearrange("(p c) o -> p (c o)", p=P), no_tok[:, :]).then_inc(lists_clear, 16)

            def load_group(n, u):
                for r, (a, c) in enumerate(zip(QPART, KPART)):
                    rows = slice(16 * r, 16 * r + 16)
                    q_src = qk_dram[0, a, bass.ds(n * 64, 64), :]
                    sp.dma_start(q_aug[u][rows], q_src.rearrange("(h d) (f t) -> d f h t", h=HG, f=2)
                                 ).then_inc(aug_in[u], 16)
                    k_src = qk_dram[1, c, bass.ds(n * 64, 64), :]
                    sp.dma_start(k_aug[u][rows], k_src.rearrange("(h d) t -> d h t", h=HG)
                                 ).then_inc(aug_in[u], 16)
                sp.dma_start(k_aug[u][96:99], alibi[bass.ds(n * 3, 3)]).then_inc(aug_in[u], 16)

            def chunk(b, f, last):
                for i in range(4):
                    sp.wait_ge(part3_s, 8 * b + 4 * f + i + 1)
                    dst = qk_dram[i // 2, :, bass.ds(b * D + (i % 2) * P, P), f * HALF:(f + 1) * HALF]
                    sp.dma_start(dst.rearrange("a p t -> p a t"),
                                 parts[:, f, i].rearrange("p (a t) -> p a t", a=3)).then_inc(parts_out[f], 16)
                if not (isinstance(b, int) and b == B - 1):
                    sp.wait_ge(xn_s, 2 * b + f + 1)
                    load_x(b + 1, f)
                if isinstance(b, int) and (b, f) == (0, 1):
                    for g in range(2):
                        sp.wait_ge(parts_out[g], 64)
                    sp.wait_ge(ones_s, 1)
                    load_group(0, 0)
                    load_group(1, 1)

            chunks_of(sp, chunk)
            for f in range(2):
                sp.wait_ge(parts_out[f], 64 * B)

            def put_maxima(n, u, half):
                sp.wait_ge(mt_sb, 2 * n + half + 1)
                for a in range(3):
                    dst = q_aug[u][KS + a:KS + a + 1, half].rearrange("o h (t q) -> o (h t) q", q=P)
                    sp.dma_start(dst, mrows[16 * a:16 * a + 16, half, :]).then_inc(m_in[half], 16)

            def group(n, u, rounds=None):
                put_maxima(n, u, 1)
                if not (isinstance(n, int) and n + 2 >= NG):
                    after(sp, st_ready, n * 24)
                    load_group(n + 2, (u + 2) % UNROLL)
                if not (isinstance(n, int) and n + 1 >= NG):
                    put_maxima(n + 1, (u + 1) % UNROLL, 0)

            put_maxima(0, 0, 0)
            groups_of(sp, group)

            sp.wait_ge(pv_s, NS * NG)
            for f in range(2):
                sp.dma_start(xr[:, f], x_rows[f * HALF:(f + 1) * HALF, :].rearrange("(t p) d -> p t d", p=P)
                             ).then_inc(xr_in[f], 16)
            for e in range(E):
                sp.dma_start(w1s[:, e].rearrange("p (c f) -> p c f", c=DC),
                             w1[e].rearrange("(c p) f -> p c f", p=P)).then_inc(w1_in, 16)
            for j in range(CH):
                f = j % 2
                sp.wait_ge(yn_s, j + 1)
                sp.wait_ge(z_s, j + 1)
                sp.wait_ge(score_s, j + 1)
                sp.dma_start(pk_rows[j], pks[:, f]).then_inc(pk_out[f], 16)
                if j + 2 < CH:
                    src = x_rows[(j + 2) * HALF:(j + 3) * HALF, :].rearrange("(t p) d -> p t d", p=P)
                    sp.dma_start(xr[:, f], src).then_inc(xr_in[f], 16)
            for e in range(E):
                if e == 0:
                    sp.wait_ge(aff_ready, CH)
                sp.dma_start(w2s[:, e].rearrange("p (c d) -> p c d", c=FC),
                             w2[e].rearrange("(c p) d -> p c d", p=P)).then_inc(w2_in, 16)
            for f in range(2):
                sp.wait_ge(pk_out[f], 16 * CH // 2)
            sp.sem_inc(packed_done, 1)
            sp.wait_ge(table_s, 1)
            sp.wait_ge(lists_done, 1)

            def load_ids(k, dst, s):
                first = sp.value_load(tile_tab[0:1, 1, bass.ds(k, 1)], min_val=0, max_val=LISTS - P)
                sp.dma_start(dst[:, :], list_dram[bass.ds(first, P), :]).then_inc(s, 16)

            for u in range(UNROLL):
                load_ids(u, ids_g[u], idg_in[u])

            def tile(k, u, it):
                after(sp, out_s[u], 16 * it)
                load_ids(k, ids_s[u], ids_in[u])
                if not (isinstance(k, int) and k + UNROLL >= TILES):
                    sp.wait_ge(gat_in[u], 16 * it + 16)
                    load_ids(k + UNROLL, ids_g[u], idg_in[u])

            tiles_of(sp, tile)
            for u in range(UNROLL):
                sp.wait_ge(out_s[u], 16 * (TILES // UNROLL))

        @block.gpsimd
        def _(pool):
            links = [0]

            def link(ins):
                links[0] += 1
                ins.then_inc(pool_chain, 1)
                pool.wait_ge(pool_chain, links[0])

            pool.memset(neg_half[:, :], -0.5)
            pool.memset(no_tok[:, :], NO_TOKEN).then_inc(fill, 1)
            pool.memset(onesB[:, :], 1.0)
            pool.memset(cum[:, 0], 0.0)
            pool.memset(cumB[:, 0], 0.0)
            for u in range(UNROLL):
                last = pool.memset(v_grp[u], 1.0)
            last.then_inc(fill, 1)

            def inv_std(f, k, s_stats, s_var, s_rstd):
                wait_apart(pool, s_stats, 2 * k)
                pool.tensor_scalar(var[:, f], mv[:, f, :, 1], EPS, None, ALU.add).then_inc(s_var, 1)
                pool.wait_ge(s_var, k)
                pool.tensor_tensor(rstd[:, f], var[:, f], neg_half[:, :], ALU.pow).then_inc(s_rstd, 1)

            inv_std(0, 1, stats, var_s, rstd_s)

            def chunk(b, f, last):
                if not last:
                    inv_std(1 - f, 2 * b + f + 2, stats, var_s, rstd_s)
                for i in range(4):
                    k = 8 * b + 4 * f + i + 1
                    pool.wait_ge(part2_s, k)
                    pool.tensor_tensor(parts[:, f, i, 2 * HALF:], resid[:, i % 2], parts[:, f, i, HALF:2 * HALF],
                                       ALU.subtract).then_inc(part3_s, 1)

            chunks_of(pool, chunk)

            def maxima_parts(n, half):
                k = 2 * n + half
                src = mx[:, 3 * half].rearrange("p h t -> p (h t)")
                v = nm[:, 0]
                r = nm[:, 1]
                if half == 0:
                    pool.wait_ge(max_s, 48 * n + 16)
                else:
                    pool.wait_ge(comb_s, n + 1)
                wait_apart(pool, mt_ready, k)
                pool.tensor_scalar(v, src, -1.0, None, ALU.mult).then_inc(mneg_s, 1)
                wait_apart(pool, mneg_s, 4 * k + 1)
                pool.tensor_copy(mparts[:, 0], v).then_inc(mneg_s, 1)
                wait_apart(pool, mneg_s, 4 * k + 2)
                pool.tensor_tensor(r, v, mparts[:, 0], ALU.subtract).then_inc(mneg_s, 1)
                wait_apart(pool, mneg_s, 4 * k + 3)
                pool.tensor_copy(mparts[:, 1], r).then_inc(mneg_s, 1)
                wait_apart(pool, mneg_s, 4 * k + 4)
                pool.tensor_tensor(mparts[:, 2], r, mparts[:, 1], ALU.subtract).then_inc(mparts_s, 1)

            def group_values(n, u):
                src = va[:, bass.ds(n * KT * 64, KT * 64)].rearrange("p (k h d) -> p k h d", k=KT, h=HG)
                pool.tensor_copy(v_grp[u][:, :, :, 0:HD], src).then_inc(vg_s, 1)

            pool.wait_ge(v_sb, 2 * CH)
            group_values(0, 0)
            maxima_parts(0, 0)
            maxima_parts(0, 1)

            def group(n, u, rounds=None):
                is_last = isinstance(n, int) and n == NG - 1
                for s in range(NS):
                    if s == 1 and not is_last:
                        wait_apart(pool, pv_s, 12 * n)
                        group_values(n + 1, (u + 1) % UNROLL)
                    if s == 5 and not is_last:
                        maxima_parts(n + 1, 0)
                if not is_last:
                    maxima_parts(n + 1, 1)

            groups_of(pool, group)

            def put_ids(j):
                f = j % 2
                pool.wait_ge(slot_s, j + 1)
                for t in range(TC):
                    pool.indirect_dma_start(
                        out=list_dram, out_offset=bass.IndirectOffsetOnAxis(ap=slot[:, f, t:t + 1], axis=0),
                        in_=slot_tok[:, f, t:t + 1], in_offset=None,
                        bounds_check=LISTS - 1, oob_is_err=False).then_inc(ids_out[f], 16)

            pool.wait_ge(lists_clear, 16)
            for j in range(CH):
                f = j % 2
                inv_std(f, 2 * j + 1, stats_c, var_c, rstd_c)
                inv_std(f, 2 * j + 2, stats_c, var_c, rstd_c)
                pool.wait_ge(y_s, j + 1)
                if j >= 2:
                    pool.wait_ge(pk_out[f], 16 * (j // 2))
                pool.tensor_tensor(pks[:, f, :, D:2 * D], x1[:, f], ys[:, f], ALU.add).then_inc(z_s, 1)
                if j >= 2:
                    put_ids(j - 2)
            put_ids(CH - 2)
            put_ids(CH - 1)
            for f in range(2):
                pool.wait_ge(ids_out[f], 16 * TC * CH // 2)
            pool.sem_inc(lists_done, 1)


            def gather(u, rounds):
                wait_apart(pool, idg_in[u], 16 * rounds)
                pool.indirect_dma_start(
                    out=gat[:, u], out_offset=None, in_=pk_dram,
                    in_offset=bass.IndirectOffsetOnAxis(ap=ids_g[u][:, 0:1], axis=0),
                    bounds_check=TOK - 1, oob_is_err=False).then_inc(gat_in[u], 16)

            pool.wait_ge(packed_done, 1)
            last = pool.memset(gat[:, :, :], 0.0)
            link(last)
            for u in range(UNROLL):
                gather(u, 1)

            def tile(k, u, it):
                wait_apart(pool, yo_s, k + 1)
                wait_apart(pool, ids_in[u], 16 * it + 16)
                pool.indirect_dma_start(
                    out=out_rows, out_offset=bass.IndirectOffsetOnAxis(ap=ids_s[u][:, 0:1], axis=0),
                    in_=yo[:, u, D:2 * D], in_offset=None,
                    bounds_check=TOK - 1, oob_is_err=False).then_inc(out_s[u], 16)
                if not (isinstance(k, int) and k + UNROLL >= TILES):
                    gather(u, it + 2)

            tiles_of(pool, tile)

        @block.scalar
        def _(act):
            def copy_xt(k, f):
                for c in range(DC):
                    act.wait_ge(xt_ready, 2 * k + c - 1)
                    act.copy(xnT[:, f, c], ps[:, c, :]).then_inc(xt_sb, 1)

            copy_xt(1, 0)
            act.wait_ge(tab_ready, 1)
            act.copy(tabT[:, :], ps[:, 6, 0:TABS]).then_inc(tab_sb, 1)

            def chunk(b, f, last):
                for i in range(4):
                    act.wait_ge(qk_ready, 8 * b + 4 * f + i + 1)
                    after(act, parts_out[f], 64 * b)
                    act.activation(parts[:, f, i, 0:HALF], ps[:, 2 + i, :], ACT.Copy,
                                   scale=HD ** -0.5 if i < 2 else 1.0).then_inc(part1_s, 1)
                if not last:
                    copy_xt(2 * b + f + 2, 1 - f)
                for w in range(2):
                    act.wait_ge(v_ready, 4 * b + 2 * f + w + 1)
                    dst = va[:, bass.ds(b * G * KT * 64, G * KT * 64)].rearrange("p (g k c) -> p k g c", g=G, k=KT)
                    k0 = 4 * f + 2 * w
                    for k in range(2):
                        last_copy = act.copy(dst[:, k0 + k],
                                             ps[:, 6 + w, k * D:(k + 1) * D].rearrange("p (g c) -> p g c", g=G))
                    last_copy.then_inc(v_sb, 1)

            chunks_of(act, chunk)

            def copy_mt(n, half):
                act.wait_ge(mt_ready, 2 * n + half + 1)
                after(act, m_in[half], 48 * n)
                act.copy(mrows[:, half, :], ps[0:48, 7, 0:P // 2].bitcast(BF16)).then_inc(mt_sb, 1)

            def copy_o(n, half):
                act.wait_ge(pv_s, 12 * n + (12 if half else 4))
                after(act, ot_ready, 2 * n + half - 1)
                act.copy(o_sb[:, half], ps[:, 6, :]).then_inc(o_sb_s, 1)

            def group(n, u, rounds=None):
                static = isinstance(n, int)
                for s in range(NS):
                    c = first_col(s)
                    for p in range(2):
                        act.wait_ge(st_ready, 24 * n + 2 * s + p + 1)
                        if p == 0:
                            after(act, pv_s, 12 * n + s - 2)
                        act.activation(probs[s % 3][:, 2 * p:2 * p + 2, c:], ps[:, 2 * p:2 * p + 2, c:],
                                       ACT.Exp).then_inc(exp_s, 1)
                        if s == 1 and p == 0:
                            copy_mt(n, 1)
                        if s == 7 and p == 0 and not (static and n == NG - 1):
                            copy_mt(n + 1, 0)
                    if s == 1 and not (static and n == 0):
                        copy_o(n - 1, 1)
                    if s == 5:
                        copy_o(n, 0)

            copy_mt(0, 0)
            groups_of(act, group)
            copy_o(NG - 1, 1)

            ao_v = ao.rearrange("p (b g t c) -> p b t g c", b=B, g=G, t=KT)

            def copy_stage(j):
                f = j % 2
                if j >= 2:
                    act.wait_ge(at_ready, j - 1)
                for t in range(TC):
                    last = act.copy(stage[:, f, t].rearrange("p (g c) -> p g c", g=G), ao_v[:, j // 2, 4 * f + t])
                last.then_inc(stage_s, 1)

            def copy_at(j):
                act.wait_ge(at_ready, j + 1)
                for c in range(DC):
                    last = act.copy(aoT[:, j % 2, c], ps[:, c, :])
                last.then_inc(at_sb, 1)

            def copy_yt(j):
                act.wait_ge(yt_ready, j + 1)
                for c in range(DC):
                    last = act.copy(yT[:, j % 2, c], ps[:, 4 + c, :])
                last.then_inc(yt_sb, 1)

            act.wait_ge(ao_s, 2 * NG)
            copy_stage(0)
            copy_at(0)
            copy_stage(1)
            for j in range(CH):
                if j + 1 < CH:
                    copy_at(j + 1)
                if j + 2 < CH:
                    copy_stage(j + 2)
                if j >= 1:
                    copy_yt(j - 1)
            copy_yt(CH - 1)

            act.wait_ge(table_s, 1)

            def expert_of(k):
                return act.value_load(tile_tab[0:1, 0, bass.ds(k, 1)], min_val=0, max_val=E - 1)

            def hidden(k):
                act.wait_ge(h_ready, 2 * k + 1)
                act.copy(hs[:, 0:HALF], ps[:, 1, :]).then_inc(h_act, 1)

            def tile(k, u, it):
                e = expert_of(k)
                act.wait_ge(gat_in[u], 16 * it + 16)
                act.activation(alph[:, u, 0:1], gat[:, u, 2 * D:2 * D + 1], ACT.Exp, scale=-1.0).then_inc(alph_s, 1)
                act.wait_ge(ht_ready, 2 * k + 1)
                for c in range(4):
                    last = act.activation(hT[:, c], ps[:, 3, c * P:(c + 1) * P], ACT.Relu,
                                          bias=tabT[:, bass.ds(e * FC + c, 1)])
                last.then_inc(ht_act, 1)
                if not (isinstance(k, int) and k == TILES - 1):
                    hidden(k + 1)

            hidden(0)
            tiles_of(act, tile)

        @block.vector
        def _(dve):
            def norm_stats(src, f, k, s_stats):
                for t in range(TC):
                    last = dve.bn_stats(st6[:, f, t], src[:, f, t])
                last.then_inc(s_stats, 1)
                wait_apart(dve, s_stats, 2 * k - 1)
                for t in range(TC):
                    last = dve.bn_aggr(mv[:, f, t], st6[:, f, t])
                last.then_inc(s_stats, 1)

            def normalise(dst, src, f, k, s_rstd, s_out):
                dve.wait_ge(s_rstd, k)
                for t in range(TC):
                    last = dve.tensor_scalar(dst(t), src[:, f, t], mv[:, f, t, 0:1], rstd[:, f, t:t + 1],
                                             ALU.subtract, ALU.mult)
                last.then_inc(s_out, 1)

            for u in range(UNROLL):
                dve.memset(q_aug[u][96:KE], 1.0)
                last = dve.memset(k_aug[u][96:KE], 1.0)
            last.then_inc(ones_s, 1)

            def layer_norm(b, f, k):
                dve.wait_ge(x_got[f], 16 * b + 16)
                norm_stats(x_in, f, k, stats)
                normalise(lambda t: xn[:, f, t], x_in, f, k, rstd_s, xn_s)

            layer_norm(0, 0, 1)

            def chunk(b, f, last):
                if not last:
                    layer_norm(b + f, 1 - f, 2 * b + f + 2)
                for i in range(4):
                    k = 8 * b + 4 * f + i + 1
                    p1 = parts[:, f, i, 0:HALF]
                    dve.wait_ge(part1_s, k)
                    after(dve, part3_s, k - 2)
                    dve.scalar_tensor_tensor(out=resid[:, i % 2], in0=ps[:, 2 + i, :],
                                             scalar=HD ** -0.5 if i < 2 else 1.0, in1=p1,
                                             op0=ALU.mult, op1=ALU.subtract).then_inc(resid_s, 1)
                    dve.wait_ge(resid_s, k)
                    dve.tensor_copy(parts[:, f, i, HALF:2 * HALF], resid[:, i % 2]).then_inc(part2_s, 1)

            chunks_of(dve, chunk)

            def maximum(n, s, h):
                t, c = CHUNKS[s]
                w = chunk_cols(s)
                k = 48 * n + 4 * s + h
                if t // 4 == c:
                    wait_apart(dve, s_ready, k + 1)
                else:
                    dve.wait_ge(s_ready, k + 1)
                src = ps[:, 4 + h % 2, 0:w]
                dst = mx[:, c + t // 4, h, t % 4:t % 4 + 1]
                if t // 4 == c:
                    dve.tensor_tensor_reduce(src, src, maskF[:, HALF - w:], 1.0, LOW,
                                             ALU.add, ALU.max, dst).then_inc(max_s, 1)
                else:
                    dve.tensor_reduce(dst, src, AX, ALU.max).then_inc(max_s, 1)

            def step_maxima(n, s):
                if s == 0:
                    after(dve, mparts_s, 2 * n - 1)
                if s == 4:
                    after(dve, mparts_s, 2 * n)
                for h in range(HG):
                    maximum(n, s, h)
                if s == NS - 1:
                    dve.wait_ge(max_s, 48 * n + 48)
                    dve.tensor_tensor(mx[:, 3], mx[:, 1], mx[:, 2], ALU.max).then_inc(comb_s, 1)

            def attention_out(n, half):
                k = 2 * n + half
                src = ps[:, 7, :].rearrange("p (t h c) -> p t h c", t=TC, h=HG)
                dve.wait_ge(ot_ready, k + 1)
                dve.reciprocal(rec[:, :, :], src[:, :, :, HD]).then_inc(rec_s, 1)
                dve.wait_ge(rec_s, k + 1)
                at = n * KT * 64 + half * TC * 64
                dst = ao[:, bass.ds(at, TC * 64)].rearrange("p (t h c) -> p t h c", t=TC, h=HG)
                dve.tensor_tensor(dst, src[:, :, :, 0:HD], rec.unsqueeze(3).broadcast_to([P, TC, HG, HD]),
                                  ALU.mult).then_inc(ao_s, 1)

            dve.wait_ge(fill, 2)
            for f in range(2):
                dve.wait_ge(parts_out[f], 64 * B)
            for s in range(NS):
                step_maxima(0, s)

            def group(n, u, rounds=None):
                static = isinstance(n, int)
                for s in range(NS):
                    if not (static and n == NG - 1):
                        step_maxima(n + 1, s)
                    if s == 4 and not (static and n == 0):
                        attention_out(n - 1, 1)
                    if s == 8:
                        attention_out(n, 0)

            groups_of(dve, group)
            attention_out(NG - 1, 1)

            links = [0]

            def link(ins):
                links[0] += 1
                ins.then_inc(dve_chain, 1)
                dve.wait_ge(dve_chain, links[0])

            def residual(j):
                f = j % 2
                dve.wait_ge(xr_in[f], 16 * (j // 2) + 16)
                dve.wait_ge(proj_ready, j + 1)
                if j >= 2:
                    dve.wait_ge(z_s, j - 1)
                for w in range(2):
                    dve.tensor_tensor(x1[:, f, 2 * w:2 * w + 2].rearrange("p t d -> p (t d)"), ps[:, 2 + w, :],
                                      xr[:, f, 2 * w:2 * w + 2].rearrange("p t d -> p (t d)"),
                                      ALU.add).then_inc(x1_s, 1)
                dve.wait_ge(x1_s, 2 * j + 2)
                norm_stats(x1, f, 2 * j + 1, stats_c)
                if j >= 2:
                    dve.wait_ge(yt_ready, j - 1)
                normalise(lambda t: ys[:, f, t], x1, f, 2 * j + 1, rstd_c, y_s)
                dve.wait_ge(y_s, j + 1)
                norm_stats(ys, f, 2 * j + 2, stats_c)
                if j >= 2:
                    dve.wait_ge(pk_out[f], 16 * (j // 2))
                normalise(lambda t: pks[:, f, t, 0:D], ys, f, 2 * j + 2, rstd_c, yn_s)

            def route(j):
                f = j % 2
                aff = ps[:, 6, 0:TC * E].rearrange("p (t e) -> p t e", t=TC)
                dve.wait_ge(aff_ready, j + 1)
                top = rs[:, 0]
                link(dve.tensor_reduce(top, aff, AX, ALU.max))
                dve.tensor_copy(pks[:, f, :, 2 * D], top).then_inc(score_s, 1)
                link(dve.tensor_tensor(rt[:, 0], aff, top.unsqueeze(2).broadcast_to([P, TC, E]), ALU.is_ge))
                prefer = cst[:, 0:E].unsqueeze(1).broadcast_to([P, TC, E])
                link(dve.tensor_tensor(rt[:, 1], rt[:, 0], prefer, ALU.mult))
                link(dve.tensor_reduce(rs[:, 1], rt[:, 1], AX, ALU.max))
                if j >= 2:
                    dve.wait_ge(rank_ready, j - 1)
                link(dve.tensor_tensor(ohB[:, f], rt[:, 1], rs[:, 1].unsqueeze(2).broadcast_to([P, TC, E]),
                                       ALU.is_equal))
                link(dve.tensor_reduce(csum[:, :], ohB[:, f].rearrange("p t e -> p e t"), AX, ALU.add))
                link(dve.tensor_tensor(cum[:, 1 - f], cum[:, f], csum[:, :], ALU.add))
                dve.tensor_copy(cumB[:, 1 - f], cum[:, 1 - f]).then_inc(oh_s, 1)

            def put_slots(j):
                f = j % 2
                rank = ps[:, 7, 0:TC * E].rearrange("p (t e) -> p t e", t=TC)
                first = cst[:, E:2 * E].unsqueeze(1).broadcast_to([P, TC, E])
                dve.wait_ge(rank_ready, j + 1)
                link(dve.tensor_tensor(rt[:, 2], rank, first, ALU.add))
                link(dve.tensor_tensor(rt[:, 3], rt[:, 2], ohB[:, f], ALU.mult))
                link(dve.tensor_reduce(rs[:, 2], rt[:, 3], AX, ALU.add))
                if j >= 2:
                    dve.wait_ge(ids_out[f], 16 * TC * (j // 2))
                dve.tensor_copy(slot[:, f], rs[:, 2])
                dve.tensor_copy(slot_tok[:, f], tok_id[:, j * TC:(j + 1) * TC]).then_inc(slot_s, 1)

            for j in range(CH):
                residual(j)
                if j >= 1:
                    route(j - 1)
                if j >= 2:
                    put_slots(j - 2)
            route(CH - 1)
            put_slots(CH - 2)
            put_slots(CH - 1)

            dve.wait_ge(count_ready, 1)
            link(dve.tensor_copy(tt[:, 0, 0:E], ps[:, 6, 0:E]))
            grid = tcmp[:, 0:E * T].rearrange("p (e k) -> p e k", e=E)
            link(dve.tensor_tensor(grid, tt[:, 0, 0:E].unsqueeze(2).broadcast_to([P, E, T]),
                                   cst[:, 16:16 + T].unsqueeze(1).broadcast_to([P, E, T]), ALU.is_gt))
            link(dve.tensor_reduce(tt[:, 1, 0:E], grid, AX, ALU.add))
            link(dve.tensor_copy(tt[:, 2, 0:E], tt[:, 1, 0:E]))
            for e in range(1, E):
                link(dve.tensor_tensor(tt[:, 2, e:e + 1], tt[:, 2, e - 1:e], tt[:, 1, e:e + 1], ALU.add))
            past = tcmp[:, 0:TILES * (E - 1)].rearrange("p (k e) -> p k e", e=E - 1)
            ends = tt[:, 2, 0:E - 1].unsqueeze(1).broadcast_to([P, TILES, E - 1])
            number = cst[:, 48:48 + TILES].unsqueeze(2).broadcast_to([P, TILES, E - 1])
            link(dve.tensor_tensor(past, number, ends, ALU.is_ge))
            link(dve.tensor_reduce(tt[:, 3, 0:TILES], past, AX, ALU.add))
            link(dve.tensor_tensor(past, past, tt[:, 1, 0:E - 1].unsqueeze(1).broadcast_to([P, TILES, E - 1]),
                                   ALU.mult))
            link(dve.tensor_reduce(tt[:, 4, 0:TILES], past, AX, ALU.add))
            link(dve.tensor_tensor(tt[:, 5, 0:TILES], cst[:, 48:48 + TILES], tt[:, 4, 0:TILES], ALU.subtract))
            link(dve.tensor_scalar(tt[:, 6, 0:TILES], tt[:, 3, 0:TILES], float(LIST), None, ALU.mult))
            link(dve.scalar_tensor_tensor(out=tt[:, 7, 0:TILES], in0=tt[:, 5, 0:TILES], scalar=float(P),
                                          in1=tt[:, 6, 0:TILES], op0=ALU.mult, op1=ALU.add))
            dve.tensor_copy(tile_tab[:, 0, 0:TILES], tt[:, 3, 0:TILES])
            dve.tensor_copy(tile_tab[:, 1, 0:TILES], tt[:, 7, 0:TILES]).then_inc(table_s, 1)
            dve.wait_ge(table_s, 1)

            def expert_of(k):
                return dve.value_load(tile_tab[0:1, 0, bass.ds(k, 1)], min_val=0, max_val=E - 1)

            def scale_shift(k, u):
                e = expert_of(k)
                dve.wait_ge(et_ready, k + 1)
                for c in range(DC):
                    last = dve.tensor_scalar(eT[:, u, c], ps[:, 0, c * P:(c + 1) * P],
                                             tabT[:, bass.ds(e * DC + (E * FC + c), 1)],
                                             tabT[:, bass.ds(e * DC + (E * (FC + DC) + c), 1)], ALU.mult, ALU.add)
                last.then_inc(et_sb, 1)

            def hidden(k):
                dve.wait_ge(h_ready, 2 * k + 2)
                dve.tensor_copy(hs[:, HALF:], ps[:, 2, :]).then_inc(h_dve, 1)

            def tile(k, u, it):
                more = not (isinstance(k, int) and k == TILES - 1)
                if more:
                    scale_shift(k + 1, (u + 1) % UNROLL)
                e = expert_of(k)
                dve.wait_ge(ht_ready, 2 * k + 2)
                for c in range(4, FC):
                    last = dve.tensor_scalar(hT[:, c], ps[:, 4, (c - 4) * P:(c - 3) * P],
                                             tabT[:, bass.ds(e * FC + c, 1)], 0.0, ALU.add, ALU.max)
                last.then_inc(ht_dve, 1)
                if more:
                    hidden(k + 1)
                dve.wait_ge(alph_s, k + 1)
                dve.tensor_scalar(alph[:, u, 1:2], alph[:, u, 0:1], 1.0, None, ALU.add).then_inc(y_chain, 1)
                dve.wait_ge(y_chain, 3 * k + 1)
                dve.reciprocal(alph[:, u, 2:3], alph[:, u, 1:2]).then_inc(y_chain, 1)
                dve.wait_ge(ye_ready, k + 1)
                after(dve, out_s[u], 16 * it)
                dve.tensor_tensor(yo[:, u, 0:D], ps[:, 5 + u, 0:D], b2r[:, bass.ds(e * D, D)],
                                  ALU.add).then_inc(y_chain, 1)
                dve.wait_ge(y_chain, 3 * k + 3)
                dve.scalar_tensor_tensor(out=yo[:, u, D:2 * D], in0=yo[:, u, 0:D], scalar=alph[:, u, 2:3],
                                         in1=gat[:, u, D:2 * D], op0=ALU.mult, op1=ALU.add).then_inc(yo_s, 1)

            scale_shift(0, 0)
            hidden(0)
            tiles_of(dve, tile)

        @block.tensor
        def _(pe):
            def transpose(dst, src, rows=P):
                return pe.transpose(dst, src, identF[0:rows, 0:rows])

            pe.wait_ge(const_in, 16 * CONSTS)

            def turn(k, f):
                pe.wait_ge(xn_s, k)
                for c in range(DC):
                    for t in range(TC):
                        last = transpose(ps[:, c, t * P:(t + 1) * P], xn[:, f, t, c * P:(c + 1) * P])
                    last.then_inc(xt_ready, 1)

            turn(1, 0)
            transpose(ps[:, 6, 0:TABS], tabs[0:TABS, :], TABS).then_inc(tab_ready, 1)
            pe.wait_ge(tab_sb, 1)

            def chunk(b, f, last):
                k = 2 * b + f + 1
                pe.wait_ge(xt_sb, 2 * k)
                for i in range(4):
                    m = (i % 2) * P
                    after(pe, resid_s, 8 * b + 4 * f + i - 3)
                    for c in range(DC):
                        mm = pe.matmul(ps[:, 2 + i, :], wqkv[:, i // 2, c, m:m + P],
                                       xnT[:, f, c], start=(c == 0), stop=(c == DC - 1))
                    mm.then_inc(qk_ready, 1)
                if not last:
                    turn(k + 1, 1 - f)
                for w in range(2):
                    after(pe, v_sb, 4 * b + 2 * f + w - 1)
                    for t in range(2):
                        for c in range(DC):
                            at = (2 * w + t) * P
                            mm = pe.matmul(ps[:, 6 + w, t * D:(t + 1) * D], xnT[:, f, c, at:at + P],
                                           wqkv[:, 2, c, :], start=(c == 0), stop=(c == DC - 1))
                    mm.then_inc(v_ready, 1)

            chunks_of(pe, chunk)

            def score_chunk(n, u, s, h):
                t, c = CHUNKS[s]
                k = 48 * n + 4 * s + h
                after(pe, max_s, k - 1)
                pe.matmul(ps[:, 4 + h % 2, 0:chunk_cols(s)],
                          q_aug[u][0:KS, t // 4, h, (t % 4) * P:(t % 4 + 1) * P],
                          k_aug[u][0:KS, h, c * HALF:c * HALF + chunk_cols(s)],
                          start=True, stop=True).then_inc(s_ready, 1)

            def turn_maxima(n, half):
                k = 2 * n + half
                pe.wait_ge(mparts_s, k + 1)
                after(pe, mt_sb, k)
                wait_apart(pe, ao_s, 2 * n - 1 if half else 2 * n - 2)
                pe.transpose(ps[0:48, 7, 0:P // 2].bitcast(BF16), mparts.rearrange("p a c -> p (a c)"),
                             identB[:, :]).then_inc(mt_ready, 1)

            def exp_scores(n, u, s, p):
                half, kt = STEPS[s]
                c = first_col(s)
                after(pe, exp_s, 24 * n + 2 * s + p - 1)
                for h in (2 * p, 2 * p + 1):
                    mm = pe.matmul(ps[:, h, c:], k_aug[u][0:KE, h, kt * P:(kt + 1) * P],
                                   q_aug[u][0:KE, half, h, c:], start=True, stop=s not in DIAG)
                    if s in DIAG:
                        mm = pe.matmul(ps[:, h, c:c + P], identB[:, :], laterB[:, :], start=False, stop=True)
                mm.then_inc(st_ready, 1)

            def values(n, u, s):
                half, kt = STEPS[s]
                c = first_col(s)
                if s == 0:
                    pe.wait_ge(vg_s, n + 1)
                if s in (0, 4):
                    after(pe, o_sb_s, 2 * n + half)
                pe.wait_ge(exp_s, 24 * n + 2 * s + 2)
                for h in range(HG):
                    mm = pe.matmul(ps[32 * h:32 * h + 32, 6, c:], v_grp[u][:, kt, h, :], probs[s % 3][:, h, c:],
                                   start=(kt == 0), stop=(s in (3, NS - 1)))
                mm.then_inc(pv_s, 1)

            def turn_output(n, half, mts):
                pe.wait_ge(o_sb_s, 2 * n + half + 1)
                after(pe, ao_s, 2 * n + half)
                pe.wait_ge(mt_sb, mts)
                for t in range(TC):
                    mm = transpose(ps[:, 7, t * P:(t + 1) * P], o_sb[:, half, t * P:(t + 1) * P])
                mm.then_inc(ot_ready, 1)

            pe.wait_ge(resid_s, 4 * CH)
            pe.wait_ge(v_sb, 2 * CH)
            pe.wait_ge(aug_in[0], 16 * AUG_DMAS)
            for s in range(NS):
                for h in range(HG):
                    score_chunk(0, 0, s, h)
                if s == 6:
                    turn_maxima(0, 0)

            def group(n, u, rounds=None):
                static = isinstance(n, int)
                rounds = n // UNROLL + 1 if static else rounds
                nxt = (u + 1) % UNROLL
                is_last = static and n == NG - 1
                for s in range(NS):
                    if s == 0:
                        pe.wait_ge(m_in[0], 48 * n + 48)
                        if not is_last:
                            r = (n + 1) // UNROLL + 1 if static else (rounds + 1 if u == 2 else rounds)
                            pe.wait_ge(aug_in[nxt], 16 * AUG_DMAS * r)
                    if s == 4:
                        pe.wait_ge(m_in[1], 48 * n + 48)
                    for p in range(2):
                        exp_scores(n, u, s, p)
                        if not is_last:
                            score_chunk(n + 1, nxt, s, 2 * p)
                            score_chunk(n + 1, nxt, s, 2 * p + 1)
                    if s >= 2:
                        values(n, u, s - 2)
                    elif not (static and n == 0):
                        values(n - 1, (u + 2) % UNROLL, NS - 2 + s)
                    if s == 0:
                        turn_maxima(n, 1)
                    if s == 3 and not (static and n == 0):
                        turn_output(n - 1, 1, 2 * n + 2)
                    if s == 6 and not is_last:
                        turn_maxima(n + 1, 0)
                    if s == 7:
                        turn_output(n, 0, 2 * n + 2 if is_last else 2 * n + 3)

            groups_of(pe, group)
            values(NG - 1, 0, NS - 2)
            values(NG - 1, 0, NS - 1)
            turn_output(NG - 1, 1, 2 * NG)

            def turn_attention(j):
                pe.wait_ge(stage_s, j + 1)
                after(pe, at_sb, j)
                for c in range(DC):
                    for t in range(TC):
                        mm = transpose(ps[:, c, t * P:(t + 1) * P], stage[:, j % 2, t, c * P:(c + 1) * P])
                mm.then_inc(at_ready, 1)

            def project(j):
                pe.wait_ge(at_sb, j + 1)
                after(pe, x1_s, 2 * j)
                for t in range(TC):
                    for c in range(DC):
                        mm = pe.matmul(ps[:, 2 + t // 2, (t % 2) * D:(t % 2 + 1) * D],
                                       aoT[:, j % 2, c, t * P:(t + 1) * P], wos[:, c, :],
                                       start=(c == 0), stop=(c == DC - 1))
                mm.then_inc(proj_ready, 1)

            def turn_y(j):
                pe.wait_ge(y_s, j + 1)
                after(pe, yt_sb, j)
                for c in range(DC):
                    for t in range(TC):
                        mm = transpose(ps[:, 4 + c, t * P:(t + 1) * P], ys[:, j % 2, t, c * P:(c + 1) * P])
                mm.then_inc(yt_ready, 1)

            cent_at = E * (FC + 2 * DC)
            centT = tabT[:, cent_at:cent_at + E * DC].rearrange("p (e c) -> p c e", c=DC)

            def affinity(j):
                pe.wait_ge(yt_sb, j + 1)
                after(pe, oh_s, j)
                for t in range(TC):
                    for c in range(DC):
                        mm = pe.matmul(ps[:, 6, t * E:(t + 1) * E],
                                       yT[:, j % 2, c, t * P:(t + 1) * P], centT[:, c, :],
                                       start=(c == 0), stop=(c == DC - 1))
                mm.then_inc(aff_ready, 1)

            def rank(j):
                f = j % 2
                pe.wait_ge(oh_s, j + 1)
                after(pe, slot_s, j)
                for t in range(TC):
                    dst = ps[:, 7, t * E:(t + 1) * E]
                    pe.matmul(dst, onesB[:, :], cumB[:, f], start=True, stop=False)
                    for q in range(t):
                        pe.matmul(dst, onesB[:, :], ohB[:, f, q], start=False, stop=False)
                    mm = pe.matmul(dst, beforeB[:, :], ohB[:, f, t], start=False, stop=True)
                mm.then_inc(rank_ready, 1)

            turn_attention(0)
            for j in range(CH + 2):
                if j < CH:
                    project(j)
                if j + 1 < CH:
                    turn_attention(j + 1)
                if 2 <= j:
                    rank(j - 2)
                if 1 <= j <= CH:
                    turn_y(j - 1)
                    affinity(j - 1)
            pe.matmul(ps[:, 6, 0:E], onesB[:, :], cumB[:, CH % 2], start=True, stop=True).then_inc(count_ready, 1)

            pe.wait_ge(table_s, 1)

            def expert_of(k):
                return pe.value_load(tile_tab[0:1, 0, bass.ds(k, 1)], min_val=0, max_val=E - 1)

            def turn_tokens(k, u, rounds):
                pe.wait_ge(gat_in[u], 16 * rounds)
                for c in range(DC):
                    mm = transpose(ps[:, 0, c * P:(c + 1) * P], gat[:, u, c * P:(c + 1) * P])
                mm.then_inc(et_ready, 1)

            w1_cols = w1s.rearrange("p e f -> p (e f)")
            w2_cols = w2s.rearrange("p e f -> p (e f)")

            def up(k, u):
                e = expert_of(k)
                pe.wait_ge(et_sb, k + 1)
                for half in range(2):
                    for c in range(DC):
                        mm = pe.matmul(ps[:, 1 + half, :], eT[:, u, c],
                                       w1_cols[:, bass.ds(e * (DC * F) + (c * F + half * HALF), HALF)],
                                       start=(c == 0), stop=(c == DC - 1))
                    mm.then_inc(h_ready, 1)

            def turn_hidden(k):
                for half, s in ((0, h_act), (1, h_dve)):
                    pe.wait_ge(s, k + 1)
                    for c in range(4):
                        at = half * HALF + c * P
                        mm = transpose(ps[:, 3 + half, c * P:(c + 1) * P], hs[:, at:at + P])
                    mm.then_inc(ht_ready, 1)

            def down(k, u):
                e = expert_of(k)
                for half, s in ((0, ht_act), (1, ht_dve)):
                    pe.wait_ge(s, k + 1)
                    for c in range(4 * half, 4 * half + 4):
                        mm = pe.matmul(ps[:, 5 + u, 0:D], hT[:, c], w2_cols[:, bass.ds(e * (FC * D) + c * D, D)],
                                       start=(c == 0), stop=(c == FC - 1))
                mm.then_inc(ye_ready, 1)

            def tile(k, u, it):
                more = not (isinstance(k, int) and k == TILES - 1)
                nxt = (u + 1) % UNROLL
                if more:
                    turn_tokens(k + 1, nxt, it + 2 if u == 2 else it + 1)
                turn_hidden(k)
                if more:
                    up(k + 1, nxt)
                down(k, u)

            turn_tokens(0, 0, 1)
            pe.wait_ge(w1_in, 16 * E)
            up(0, 0)
            pe.wait_ge(w2_in, 16 * E)
            tiles_of(pe, tile)


def shape_constants():
    import numpy as np

    bf16 = mybir.dt.np(BF16)
    eye = np.eye(P, dtype=np.float32)
    before = np.triu(np.ones((P, P), np.float32), 1).astype(bf16)
    later = np.tril(np.full((P, P), LOW, np.float32), -1).astype(bf16)
    mask = np.zeros((P, HALF), np.float32)
    mask[:, HALF - P:] = np.triu(np.full((P, P), LOW, np.float32), 1)
    slope = np.array([2.0 ** (-8.0 / H * (i + 1)) for i in range(H)], np.float32)
    rest = slope[:, None] * np.arange(L, dtype=np.float32)[None, :]
    parts = []
    for _ in range(3):
        part = rest.astype(bf16)
        parts.append(part)
        rest = rest - part.astype(np.float32)
    alibi = np.stack(parts).reshape(3, G, HG, L).transpose(1, 0, 2, 3).reshape(G * 3, HG, L)
    alibi = np.ascontiguousarray(np.tile(alibi, (B, 1, 1)))
    tokens = np.ascontiguousarray(np.arange(TOK, dtype=np.int32).reshape(T, P).T)
    row = np.zeros(96, np.float32)
    row[0:E] = E - np.arange(E)
    row[E:2 * E] = LIST * np.arange(E)
    row[16:16 + T] = P * np.arange(T)
    row[48:48 + TILES] = np.arange(TILES)
    consts = np.ascontiguousarray(np.broadcast_to(row, (P, 96)))
    return {"ident": eye, "identh": eye.astype(bf16), "before": before, "later": later, "mask": mask,
            "alibi": alibi, "tokens": tokens, "consts": consts}


_INS = ["L0_attn_x", "L0_attn_q_w", "L0_attn_k_w", "L0_attn_v_w", "L0_attn_o_w", "L0_ffn_centroids",
        "L0_ffn_ln_g", "L0_ffn_ln_b", "L0_ffn_w1", "L0_ffn_b1", "L0_ffn_w2", "L0_ffn_b2"]


def kernel(**inputs):
    import numpy as _np
    import concourse.bacc as _bacc
    from concourse import mybir as _mybir
    from concourse.bass_utils import run_bass_kernel_spmd as _run

    nc = _bacc.Bacc("TRN2", target_bir_lowering=False, num_devices=1)
    arrays, args = {}, []
    data = {name: _np.ascontiguousarray(inputs[name]) for name in _INS}
    data.update(shape_constants())
    for name, a in data.items():
        arrays[f"in_{name}_dram"] = a
        args.append(nc.dram_tensor(f"in_{name}_dram", a.shape, _mybir.dt.from_np(a.dtype), kind="ExternalInput").ap())
    args.append(nc.dram_tensor("out_0_dram", (B, L, D), _mybir.dt.float32, kind="ExternalOutput").ap())
    layer_kernel(nc, *args)
    r = _run(nc, [arrays], core_ids=[0])
    return r.results[0]["out_0_dram"]
```

```python
from contextlib import ExitStack

import concourse.bass as bass
from concourse import mybir


P = 128
B, L, D = 4, 1024, 256
H, HD = 16, 16
G = 4
HG = H // G
NG = B * G
KT = L // P
HALF = L // 2
F, E = 1024, 8
DC, FC = D // P, F // P
TOK = B * L
T = TOK // P
CH = TOK // HALF
TC = HALF // P
TILES = T + E - 1
LIST = TOK
LISTS = E * LIST + E * P
NO_TOKEN = 1 << 20
PK = 2 * D + 1
EPS = 1e-5
TABS = E * (FC + 3 * DC)
LOW = -3.0e38
UNROLL = 3
KS, KE = 99, 102
QPART = (0, 0, 0, 1, 1, 2)
KPART = (0, 1, 2, 0, 1, 0)

ALU = mybir.AluOpType
ACT = mybir.ActivationFunctionType
F32, BF16, I32 = mybir.dt.float32, mybir.dt.bfloat16, mybir.dt.int32
AX = mybir.AxisListType.X

STEPS = [(0, k) for k in range(4)] + [(1, k) for k in range(8)]
NS = len(STEPS)
CHUNKS = [(3, 0), (1, 0), (2, 0), (0, 0),
          (6, 1), (5, 1), (7, 0), (7, 1), (6, 0), (5, 0), (4, 0), (4, 1)]


def first_col(s):
    half, kt = STEPS[s]
    return max(kt * P - half * HALF, 0)


def chunk_cols(s):
    t, c = CHUNKS[s]
    return min(HALF, (t + 1) * P - c * HALF)


def score_bank(n, s, h):
    if isinstance(n, int) and n == 0:
        return h % 2 if s < 3 else h
    return 4 + h % 2


def proj_bank(j):
    return 4 if j == 0 else 2


def on_diagonal(s):
    half, kt = STEPS[s]
    return kt // 4 == half


OUT_AT = (11, 5)
DIAG = [s for s in range(NS) if on_diagonal(s)]


def layer_kernel(nc, x, wq, wk, wv, wo, cent, ln_g, ln_b, w1, b1, w2, b2,
                 ident, identh, before, later, mask, alibi, ones, tokens, consts, out):
    ctx = ExitStack()

    def sb(name, shape, dt):
        return ctx.enter_context(nc.sbuf_tensor(name, shape, dt))

    def sem(name):
        return ctx.enter_context(nc.semaphore(name))

    with ctx:
        qk_dram = nc.dram_tensor("qk_parts", [2, 3, B * D, L], BF16).ap()
        pk_dram = nc.dram_tensor("packed_tokens", [TOK, PK], F32).ap()
        list_dram = nc.dram_tensor("expert_lists", [LISTS, 1], I32).ap()

        identF = sb("identF", [P, P], F32)
        identB = sb("identB", [P, P], BF16)
        beforeB = sb("beforeB", [P, P], BF16)
        laterB = sb("laterB", [P, P], BF16)
        onesB = sb("onesB", [P, P], BF16)
        maskF = sb("maskF", [P, HALF], F32)
        wqkv = sb("wqkv", [P, 3, DC, D], F32)
        wos = sb("wos", [P, DC, D], F32)
        tok_id = sb("tok_id", [P, T], I32)
        cst = sb("cst", [P, 96], F32)
        no_tok = sb("no_tok", [P, LISTS // P], I32)
        tabs = sb("tabs", [P, P], F32)
        tabT = sb("tabT", [P, TABS], F32)
        b2r = sb("b2r", [P, E * D], F32)
        neg_half = sb("neg_half", [P, TC], F32)
        mx = sb("mx", [P, 4, HG, TC], F32)
        nm = sb("nm", [P, 2, HG * TC], F32)
        mparts = sb("mparts", [P, 3, HG * TC], BF16)
        mrows = sb("mrows", [3 * HG * TC, 2, P], BF16)
        cum = sb("cum", [P, 2, E], F32)
        cumB = sb("cumB", [P, 2, E], BF16)
        rt = sb("rt", [P, 4, TC, E], F32)
        rs = sb("rs", [P, 4, TC], F32)
        csum = sb("csum", [P, E], F32)
        ohB = sb("ohB", [P, 2, TC, E], BF16)
        slot = sb("slot", [P, 2, TC], I32)
        slot_tok = sb("slot_tok", [P, 2, TC], I32)
        tcmp = sb("tcmp", [P, 40 * 8], F32)
        tt = sb("tt", [P, 8, 40], F32)
        tile_tab = sb("tile_tab", [P, 2, 40], I32)
        st6 = sb("st6", [P, 2, TC, 6], F32)
        mv = sb("mv", [P, 2, TC, 2], F32)
        var = sb("var", [P, 2, TC], F32)
        rstd = sb("rstd", [P, 2, TC], F32)
        ids_g = [sb(f"ids_g{u}", [P, 1], I32) for u in range(UNROLL)]
        ids_s = [sb(f"ids_s{u}", [P, 1], I32) for u in range(UNROLL)]
        alph = sb("alph", [P, UNROLL, 3], F32)

        ARENA = 43 * 1024
        arena = sb("arena", [P, ARENA], F32)

        def carve(at, shape, dt=F32):
            n = 1
            for d in shape:
                n *= d
            cols = n if dt == F32 else n // 2
            assert at + cols <= ARENA, (at, cols)
            v = arena[:, at:at + cols]
            if dt != F32:
                v = v.bitcast(dt)
            if len(shape) == 2:
                v = v.rearrange("p (a b) -> p a b", a=shape[0])
            elif len(shape) == 3:
                v = v.rearrange("p (a b c) -> p a b c", a=shape[0], b=shape[1])
            return v, at + cols

        va, p0 = carve(0, [NG * KT * 64])
        q_aug, k_aug, v_grp, probs = [], [], [], []
        for u in range(UNROLL):
            v, p0 = carve(p0, [2, HG, HALF], BF16)
            q_aug.append(v)
            v, p0 = carve(p0, [HG, L], BF16)
            k_aug.append(v)
        x_in, a0 = carve(p0, [2, TC, D])
        xn, a0 = carve(a0, [2, TC, D])
        xnT, a0 = carve(a0, [2, DC, HALF])
        p1 = p0
        for u in range(UNROLL):
            v, p1 = carve(p1, [HG, HALF])
            probs.append(v)
        assert a0 <= p1
        for u in range(UNROLL):
            v, p1 = carve(p1, [KT, HG, 32])
            v_grp.append(v)
        o_sb, p1 = carve(p1, [2, HALF])
        rec, p1 = carve(p1, [TC, HG])
        ao, a1 = carve(p1, [NG * KT * 64])
        ao_v = ao.rearrange("p (b g t c) -> p b t g c", b=B, g=G, t=KT)
        parts, a0 = carve(p1, [2, 4, 3 * HALF], BF16)
        resid, a0 = carve(a0, [2, HALF])

        w1s, w2_at = carve(0, [E, DC * F])
        stage, c0 = carve(w2_at, [2, TC, D])
        aoT, c0 = carve(c0, [2, DC, HALF])
        xr, c0 = carve(c0, [2, TC, D])
        x1, c0 = carve(c0, [2, TC, D])
        ys, c0 = carve(c0, [2, TC, D])
        yT, c0 = carve(c0, [2, DC, HALF])
        assert c0 <= p1
        pks, c0 = carve(a1, [2, TC, PK])

        w2s, d0 = carve(w2_at, [E, FC * D])
        gat, d0 = carve(d0, [UNROLL, PK])
        eT, d0 = carve(d0, [UNROLL, DC, P])
        hs, d0 = carve(d0, [F])
        hT, d0 = carve(d0, [FC, P])
        yo, d0 = carve(d0, [UNROLL, 2 * D])

        ps = ctx.enter_context(nc.psum_tensor("ps", [P, 8, HALF], F32))

        weights_in = sem("weights_in")
        CONSTS = 14
        const_in = sem("const_in")
        apart = sem("apart")
        fill = sem("fill")
        tab_ready, tab_sb = sem("tab_ready"), sem("tab_sb")
        lists_clear = sem("lists_clear")
        x_got = [sem(f"x_got{f}") for f in range(2)]
        stats = sem("stats")
        var_s = sem("var_s")
        rstd_s = sem("rstd_s")
        xn_s = sem("xn_s")
        xt_ready = sem("xt_ready")
        xt_sb = sem("xt_sb")
        qk_ready = sem("qk_ready")
        part1_s = sem("part1_s")
        resid_s = sem("resid_s")
        part2_s = sem("part2_s")
        part3_s = sem("part3_s")
        parts_out = [sem(f"parts_out{f}") for f in range(2)]
        v_ready = sem("v_ready")
        v_sb = sem("v_sb")
        aug_in = [sem(f"aug_in{u}") for u in range(UNROLL)]
        vg_s = sem("vg_s")
        s_ready = sem("s_ready")
        max_s = sem("max_s")
        comb_s = sem("comb_s")
        mneg_s = sem("mneg_s")
        mparts_s = sem("mparts_s")
        mt_ready = sem("mt_ready")
        mt_sb = sem("mt_sb")
        m_in = [sem(f"m_in{h}") for h in range(2)]
        st_ready = sem("st_ready")
        exp_s = sem("exp_s")
        pv_s = sem("pv_s")
        o_sb_s = sem("o_sb_s")
        ot_ready = sem("ot_ready")
        rec_s = sem("rec_s")
        ao_s = sem("ao_s")
        xr_in = [sem(f"xr_in{f}") for f in range(2)]
        w1_in, w2_in = sem("w1_in"), sem("w2_in")
        stage_s = sem("stage_s")
        at_ready = sem("at_ready")
        at_sb = sem("at_sb")
        proj_ready = sem("proj_ready")
        x1_s = sem("x1_s")
        dve_chain = sem("dve_chain")
        y_s = sem("y_s")
        yn_s = sem("yn_s")
        z_s = sem("z_s")
        var_c, rstd_c = sem("var_c"), sem("rstd_c")
        stats_c = sem("stats_c")
        yt_ready, yt_sb = sem("yt_ready"), sem("yt_sb")
        aff_ready = sem("aff_ready")
        score_s = sem("score_s")
        oh_s = sem("oh_s")
        rank_ready = sem("rank_ready")
        slot_s = sem("slot_s")
        ids_out = [sem(f"ids_out{f}") for f in range(2)]
        pk_out = [sem(f"pk_out{f}") for f in range(2)]
        lists_done = sem("lists_done")
        packed_done = sem("packed_done")
        count_ready = sem("count_ready")
        table_s = sem("table_s")
        gat_clear = sem("gat_clear")
        idg_in = [sem(f"idg_in{u}") for u in range(UNROLL)]
        ids_in = [sem(f"ids_in{u}") for u in range(UNROLL)]
        gat_in = [sem(f"gat_in{u}") for u in range(UNROLL)]
        et_ready, et_sb = sem("et_ready"), sem("et_sb")
        h_ready = sem("h_ready")
        h_act, h_dve = sem("h_act"), sem("h_dve")
        ht_ready = sem("ht_ready")
        ht_act, ht_dve = sem("ht_act"), sem("ht_dve")
        ye_ready = sem("ye_ready")
        alph_s = sem("alph_s")
        yo_s = sem("yo_s")
        y_chain = sem("y_chain")
        out_s = [sem(f"out_s{u}") for u in range(UNROLL)]

        x_rows = x.rearrange("b l d -> (b l) d")
        out_rows = out.rearrange("b l d -> (b l) d")
        pk_rows = pk_dram.rearrange("(j t p) c -> j p t c", t=TC, p=P)
        AUG_DMAS = 2 * len(QPART) + 1

        def after(eng, s, value):
            if not (isinstance(value, int) and value <= 0):
                eng.wait_ge(s, value)

        def wait_apart(eng, s, value):
            after(eng, s, value)
            if not isinstance(value, int):
                eng.sem_inc(apart, 1)

        def chunks_of(eng, body):
            body(0, 0, False)
            body(0, 1, False)
            with eng.Fori(1, B - 1) as b:
                body(b, 0, False)
                body(b, 1, False)
            body(B - 1, 0, False)
            body(B - 1, 1, True)

        def groups_of(eng, body):
            body(0, 0)
            with eng.Fori(0, 4) as it:
                for i in range(UNROLL):
                    body(it * UNROLL + (1 + i), (1 + i) % UNROLL, rounds=it + 2 if i == 2 else it + 1)
            for n in range(NG - 3, NG):
                body(n, n % UNROLL)

        def tiles_of(eng, body):
            for u in range(UNROLL):
                body(u, u, 0)
            with eng.Fori(1, TILES // UNROLL - 1) as it:
                for u in range(UNROLL):
                    body(it * UNROLL + u, u, it)
            for u in range(UNROLL):
                body(TILES - UNROLL + u, u, TILES // UNROLL - 1)

        block = ctx.enter_context(nc.Block())

        @block.sync
        def _(sp):
            def load_x(b, f):
                src = x_rows[bass.ds(b * L + f * HALF, HALF), :].rearrange("(t p) d -> p t d", p=P)
                sp.dma_start(x_in[:, f], src).then_inc(x_got[f], 16)

            load_x(0, 0)
            sp.dma_start(identF[:, :], ident).then_inc(weights_in, 16)
            for i, w in enumerate((wq, wk, wv)):
                sp.dma_start(wqkv[:, i], w.rearrange("(c p) n -> p c n", p=P)).then_inc(weights_in, 16)
            load_x(0, 1)
            for at, t in ((0, b1), (E * FC, ln_g), (E * (FC + DC), ln_b), (E * (FC + 2 * DC), cent)):
                rows = t.rearrange("e (c p) -> (e c) p", p=P)
                sp.dma_start(tabs[at:at + rows.shape[0], :], rows).then_inc(weights_in, 16)
            sp.dma_start(wos[:, :, :], wo.rearrange("(c p) n -> p c n", p=P)).then_inc(const_in, 16)
            sp.dma_start(identB[:, :], identh).then_inc(const_in, 16)
            sp.dma_start(beforeB[:, :], before).then_inc(const_in, 16)
            sp.dma_start(laterB[:, :], later).then_inc(const_in, 16)
            sp.dma_start(maskF[:, :], mask).then_inc(const_in, 16)
            sp.dma_start(tok_id[:, :], tokens).then_inc(const_in, 16)
            sp.dma_start(cst[:, :], consts).then_inc(const_in, 16)
            b2row = b2.rearrange("(o e) d -> o (e d)", o=1)
            sp.dma_start(b2r[:, :], b2row.broadcast_to([P, E * D])).then_inc(const_in, 16)
            for u in range(UNROLL):
                sp.dma_start(q_aug[u][96:KS], ones.rearrange("r (f h t) -> r f h t", f=2, h=HG)).then_inc(const_in, 16)
                sp.dma_start(k_aug[u][KS:KE], ones.rearrange("r (h t) -> r h t", h=HG)).then_inc(const_in, 16)
            sp.wait_ge(fill, 1)
            sp.dma_start(list_dram.rearrange("(p c) o -> p (c o)", p=P), no_tok[:, :]).then_inc(lists_clear, 16)

            def load_group(n, u):
                for r, (a, c) in enumerate(zip(QPART, KPART)):
                    rows = slice(16 * r, 16 * r + 16)
                    q_src = qk_dram[0, a, bass.ds(n * 64, 64), :]
                    sp.dma_start(q_aug[u][rows], q_src.rearrange("(h d) (f t) -> d f h t", h=HG, f=2)
                                 ).then_inc(aug_in[u], 16)
                    k_src = qk_dram[1, c, bass.ds(n * 64, 64), :]
                    sp.dma_start(k_aug[u][rows], k_src.rearrange("(h d) t -> d h t", h=HG)
                                 ).then_inc(aug_in[u], 16)
                sp.dma_start(k_aug[u][96:99], alibi[bass.ds(n * 3, 3)]).then_inc(aug_in[u], 16)

            def chunk(b, f, last):
                if not (isinstance(b, int) and b == B - 1):
                    sp.wait_ge(xn_s, 2 * b + f + 1)
                    load_x(b + 1, f)
                for i in range(4):
                    sp.wait_ge(part3_s, 8 * b + 4 * f + i + 1)
                    dst = qk_dram[i // 2, :, bass.ds(b * D + (i % 2) * P, P), f * HALF:(f + 1) * HALF]
                    sp.dma_start(dst.rearrange("a p t -> p a t"),
                                 parts[:, f, i].rearrange("p (a t) -> p a t", a=3)).then_inc(parts_out[f], 16)
                if isinstance(b, int) and (b, f) == (0, 1):
                    for g in range(2):
                        sp.wait_ge(parts_out[g], 64)
                    load_group(0, 0)

            chunks_of(sp, chunk)
            load_group(1, 1)
            for f in range(2):
                sp.wait_ge(parts_out[f], 64 * B)

            def put_maxima(n, u, half):
                sp.wait_ge(mt_sb, 2 * n + half + 1)
                for a in range(3):
                    dst = q_aug[u][KS + a:KS + a + 1, half].rearrange("o h (t q) -> o (h t) q", q=P)
                    sp.dma_start(dst, mrows[16 * a:16 * a + 16, half, :]).then_inc(m_in[half], 16)

            def group(n, u, rounds=None):
                put_maxima(n, u, 1)
                if not (isinstance(n, int) and n + 2 >= NG):
                    after(sp, st_ready, n * 24)
                    load_group(n + 2, (u + 2) % UNROLL)
                if not (isinstance(n, int) and n + 1 >= NG):
                    put_maxima(n + 1, (u + 1) % UNROLL, 0)

            put_maxima(0, 0, 0)
            groups_of(sp, group)

            sp.wait_ge(pv_s, NS * NG)
            for f in range(2):
                sp.dma_start(xr[:, f], x_rows[f * HALF:(f + 1) * HALF, :].rearrange("(t p) d -> p t d", p=P)
                             ).then_inc(xr_in[f], 16)
            def load_w1(e):
                sp.dma_start(w1s[:, e].rearrange("p (c f) -> p c f", c=DC),
                             w1[e].rearrange("(c p) f -> p c f", p=P)).then_inc(w1_in, 16)

            def load_w2(e, halves=(0, 1)):
                c0, c1 = FC // 2 * halves[0], FC // 2 * (halves[-1] + 1)
                sp.dma_start(w2s[:, e, c0 * D:c1 * D].rearrange("p (c d) -> p c d", d=D),
                             w2[e, c0 * P:c1 * P].rearrange("(c p) d -> p c d", p=P)).then_inc(w2_in, 16)

            sp.wait_ge(ot_ready, 2 * NG)
            load_w1(0)
            for j in range(CH + 1):
                if j < CH:
                    sp.wait_ge(x1_s, 2 * j + 2)
                if j + 2 < CH:
                    src = x_rows[(j + 2) * HALF:(j + 3) * HALF, :].rearrange("(t p) d -> p t d", p=P)
                    sp.dma_start(xr[:, j % 2], src).then_inc(xr_in[j % 2], 16)
                if j == 0:
                    load_w1(1)
                    load_w2(6)
                elif j < CH // 2:
                    load_w1(2 * j)
                    load_w1(2 * j + 1)
                if j == CH // 2:
                    sp.wait_ge(stage_s, 2)
                    load_w2(7)
                if j == CH - 2:
                    load_w2(2, (0,))
                    sp.wait_ge(at_ready, CH)
                    load_w2(0)
                if j == CH - 1:
                    load_w2(2, (1,))
                    sp.wait_ge(proj_ready, CH)
                    load_w2(1)
                if j >= 1:
                    sp.wait_ge(yn_s, j)
                    sp.wait_ge(z_s, j)
                    sp.wait_ge(score_s, j)
                    sp.dma_start(pk_rows[j - 1], pks[:, (j - 1) % 2]).then_inc(pk_out[(j - 1) % 2], 16)
                if j == CH - 1:
                    load_w2(3, (0,))
                    load_w2(4, (0,))
                    load_w2(5, (0,))
            for f in range(2):
                sp.wait_ge(pk_out[f], 16 * CH // 2)
            sp.sem_inc(packed_done, 1)
            sp.wait_ge(table_s, 1)
            sp.wait_ge(lists_done, 1)

            def load_ids(k, dst, s):
                first = sp.value_load(tile_tab[0:1, 1, bass.ds(k, 1)], min_val=0, max_val=LISTS - P)
                sp.dma_start(dst[:, :], list_dram[bass.ds(first, P), :]).then_inc(s, 16)

            for u in range(UNROLL):
                load_ids(u, ids_g[u], idg_in[u])
            sp.wait_ge(aff_ready, CH)
            sp.wait_ge(gat_in[0], 16)
            load_w2(3, (1,))
            load_w2(4, (1,))
            load_w2(5, (1,))

            def tile(k, u, it):
                after(sp, out_s[u], 16 * it)
                load_ids(k, ids_s[u], ids_in[u])
                if not (isinstance(k, int) and k + UNROLL >= TILES):
                    sp.wait_ge(gat_in[u], 16 * it + 16)
                    load_ids(k + UNROLL, ids_g[u], idg_in[u])

            tiles_of(sp, tile)
            for u in range(UNROLL):
                sp.wait_ge(out_s[u], 16 * (TILES // UNROLL))

        @block.gpsimd
        def _(pool):
            pool.memset(neg_half[:, :], -0.5)
            pool.memset(no_tok[:, :], NO_TOKEN).then_inc(fill, 1)
            pool.memset(onesB[:, :], 1.0)
            pool.memset(cum[:, 0], 0.0)
            pool.memset(cumB[:, 0], 0.0)
            for u in range(UNROLL):
                last = pool.memset(v_grp[u], 1.0)
            last.then_inc(fill, 1)

            def inv_std(f, k, s_stats, s_var, s_rstd):
                wait_apart(pool, s_stats, 2 * k)
                pool.tensor_scalar(var[:, f], mv[:, f, :, 1], EPS, None, ALU.add).then_inc(s_var, 1)
                pool.wait_ge(s_var, k)
                pool.tensor_tensor(rstd[:, f], var[:, f], neg_half[:, :], ALU.pow).then_inc(s_rstd, 1)

            inv_std(0, 1, stats, var_s, rstd_s)

            def chunk(b, f, last):
                if not last:
                    inv_std(1 - f, 2 * b + f + 2, stats, var_s, rstd_s)
                for i in range(4):
                    k = 8 * b + 4 * f + i + 1
                    pool.wait_ge(part2_s, k)
                    pool.tensor_tensor(parts[:, f, i, 2 * HALF:], resid[:, i % 2], parts[:, f, i, HALF:2 * HALF],
                                       ALU.subtract).then_inc(part3_s, 1)

            chunks_of(pool, chunk)

            def maxima_parts(n, half):
                k = 2 * n + half
                src = mx[:, 3 * half].rearrange("p h t -> p (h t)")
                v = nm[:, 0]
                r = nm[:, 1]
                if half == 0:
                    pool.wait_ge(max_s, 48 * n + 16)
                else:
                    pool.wait_ge(comb_s, n + 1)
                wait_apart(pool, mt_ready, k)
                pool.tensor_scalar(v, src, -1.0, None, ALU.mult).then_inc(mneg_s, 1)
                wait_apart(pool, mneg_s, 4 * k + 1)
                pool.tensor_copy(mparts[:, 0], v).then_inc(mneg_s, 1)
                wait_apart(pool, mneg_s, 4 * k + 2)
                pool.tensor_tensor(r, v, mparts[:, 0], ALU.subtract).then_inc(mneg_s, 1)
                wait_apart(pool, mneg_s, 4 * k + 3)
                pool.tensor_copy(mparts[:, 1], r).then_inc(mneg_s, 1)
                wait_apart(pool, mneg_s, 4 * k + 4)
                pool.tensor_tensor(mparts[:, 2], r, mparts[:, 1], ALU.subtract).then_inc(mparts_s, 1)

            def group_values(n, u):
                src = va[:, bass.ds(n * KT * 64, KT * 64)].rearrange("p (k h d) -> p k h d", k=KT, h=HG)
                pool.tensor_copy(v_grp[u][:, :, :, 0:HD], src).then_inc(vg_s, 1)

            pool.wait_ge(v_sb, 2 * CH)
            group_values(0, 0)
            maxima_parts(0, 0)
            maxima_parts(0, 1)

            def group(n, u, rounds=None):
                is_last = isinstance(n, int) and n == NG - 1
                for s in range(NS):
                    if s == 1 and not is_last:
                        wait_apart(pool, pv_s, 12 * n)
                        group_values(n + 1, (u + 1) % UNROLL)
                    if s == 5 and not is_last:
                        maxima_parts(n + 1, 0)
                if not is_last:
                    maxima_parts(n + 1, 1)

            groups_of(pool, group)

            def put_ids(j):
                f = j % 2
                pool.wait_ge(slot_s, j + 1)
                for t in range(TC):
                    pool.indirect_dma_start(
                        out=list_dram, out_offset=bass.IndirectOffsetOnAxis(ap=slot[:, f, t:t + 1], axis=0),
                        in_=slot_tok[:, f, t:t + 1], in_offset=None,
                        bounds_check=LISTS - 1, oob_is_err=False).then_inc(ids_out[f], 16)

            pool.wait_ge(lists_clear, 16)

            def add_y(j):
                f = j % 2
                pool.wait_ge(y_s, j + 1)
                if j >= 2:
                    pool.wait_ge(pk_out[f], 16 * (j // 2))
                pool.tensor_tensor(pks[:, f, :, D:2 * D], x1[:, f], ys[:, f], ALU.add).then_inc(z_s, 1)

            for j in range(CH):
                inv_std(j % 2, 2 * j + 1, stats_c, var_c, rstd_c)
                if j >= 1:
                    add_y(j - 1)
                inv_std(j % 2, 2 * j + 2, stats_c, var_c, rstd_c)
                if j >= 1:
                    put_ids(j - 1)
            add_y(CH - 1)
            put_ids(CH - 1)
            for f in range(2):
                pool.wait_ge(ids_out[f], 16 * TC * CH // 2)
            pool.sem_inc(lists_done, 1)


            def gather(u, rounds):
                wait_apart(pool, idg_in[u], 16 * rounds)
                pool.indirect_dma_start(
                    out=gat[:, u], out_offset=None, in_=pk_dram,
                    in_offset=bass.IndirectOffsetOnAxis(ap=ids_g[u][:, 0:1], axis=0),
                    bounds_check=TOK - 1, oob_is_err=False).then_inc(gat_in[u], 16)

            pool.wait_ge(packed_done, 1)
            pool.wait_ge(gat_clear, 1)
            for u in range(UNROLL):
                gather(u, 1)

            def tile(k, u, it):
                wait_apart(pool, yo_s, k + 1)
                if not (isinstance(k, int) and k + UNROLL >= TILES):
                    gather(u, it + 2)
                wait_apart(pool, ids_in[u], 16 * it + 16)
                pool.indirect_dma_start(
                    out=out_rows, out_offset=bass.IndirectOffsetOnAxis(ap=ids_s[u][:, 0:1], axis=0),
                    in_=yo[:, u, D:2 * D], in_offset=None,
                    bounds_check=TOK - 1, oob_is_err=False).then_inc(out_s[u], 16)

            tiles_of(pool, tile)

        @block.scalar
        def _(act):
            def copy_xt(k, f):
                for c in range(DC):
                    act.wait_ge(xt_ready, 2 * k + c - 1)
                    act.copy(xnT[:, f, c], ps[:, c, :]).then_inc(xt_sb, 1)

            copy_xt(1, 0)
            act.wait_ge(tab_ready, 1)
            act.copy(tabT[:, :], ps[:, 6, 0:TABS]).then_inc(tab_sb, 1)

            def chunk(b, f, last):
                for i in range(4):
                    act.wait_ge(qk_ready, 8 * b + 4 * f + i + 1)
                    after(act, parts_out[f], 64 * b)
                    act.activation(parts[:, f, i, 0:HALF], ps[:, 2 + i, :], ACT.Copy,
                                   scale=HD ** -0.5 if i < 2 else 1.0).then_inc(part1_s, 1)
                if not last:
                    copy_xt(2 * b + f + 2, 1 - f)
                for w in range(2):
                    act.wait_ge(v_ready, 4 * b + 2 * f + w + 1)
                    dst = va[:, bass.ds(b * G * KT * 64, G * KT * 64)].rearrange("p (g k c) -> p k g c", g=G, k=KT)
                    k0 = 4 * f + 2 * w
                    for k in range(2):
                        last_copy = act.copy(dst[:, k0 + k],
                                             ps[:, 6 + w, k * D:(k + 1) * D].rearrange("p (g c) -> p g c", g=G))
                    last_copy.then_inc(v_sb, 1)

            chunks_of(act, chunk)

            def copy_mt(n, half):
                act.wait_ge(mt_ready, 2 * n + half + 1)
                after(act, m_in[half], 48 * n)
                act.copy(mrows[:, half, :], ps[0:48, 7, 0:P // 2].bitcast(BF16)).then_inc(mt_sb, 1)

            def copy_o(n, half):
                act.wait_ge(pv_s, 12 * n + (12 if half else 4))
                after(act, ot_ready, 2 * n + half - 1)
                act.copy(o_sb[:, half], ps[:, 6, :]).then_inc(o_sb_s, 1)

            def group(n, u, rounds=None):
                static = isinstance(n, int)
                for s in range(NS):
                    c = first_col(s)
                    for p in range(2):
                        act.wait_ge(st_ready, 24 * n + 2 * s + p + 1)
                        if p == 0:
                            after(act, pv_s, 12 * n + s - 2)
                        act.activation(probs[s % 3][:, 2 * p:2 * p + 2, c:], ps[:, 2 * p:2 * p + 2, c:],
                                       ACT.Exp).then_inc(exp_s, 1)
                        if s == 1 and p == 0:
                            copy_mt(n, 1)
                            if not (static and n == 0):
                                copy_o(n - 1, 1)
                        if s == 5 and p == 0:
                            copy_o(n, 0)
                        if s == 7 and p == 0 and not (static and n == NG - 1):
                            copy_mt(n + 1, 0)

            copy_mt(0, 0)
            groups_of(act, group)
            copy_o(NG - 1, 1)


            def copy_stage(j):
                f = j % 2
                if j >= 2:
                    act.wait_ge(at_ready, j - 1)
                for t in range(TC):
                    last = act.copy(stage[:, f, t].rearrange("p (g c) -> p g c", g=G), ao_v[:, j // 2, 4 * f + t])
                last.then_inc(stage_s, 1)

            def copy_at(j):
                act.wait_ge(at_ready, j + 1)
                for c in range(DC):
                    last = act.copy(aoT[:, j % 2, c], ps[:, c, :])
                last.then_inc(at_sb, 1)

            def copy_yt(j):
                act.wait_ge(yt_ready, j + 1)
                for c in range(DC):
                    last = act.copy(yT[:, j % 2, c], ps[:, 4 + c, :])
                last.then_inc(yt_sb, 1)

            act.wait_ge(ao_s, 2 * NG)
            copy_stage(1)
            copy_at(1)
            copy_stage(2)
            for j in range(CH):
                copy_yt(j)
                if j + 2 < CH:
                    copy_at(j + 2)
                if j + 3 < CH:
                    copy_stage(j + 3)

            act.wait_ge(table_s, 1)

            def expert_of(k):
                return act.value_load(tile_tab[0:1, 0, bass.ds(k, 1)], min_val=0, max_val=E - 1)

            def hidden(k):
                act.wait_ge(h_ready, 2 * k + 1)
                act.copy(hs[:, 0:HALF], ps[:, 1, :]).then_inc(h_act, 1)

            def tile(k, u, it):
                e = expert_of(k)
                act.wait_ge(gat_in[u], 16 * it + 16)
                act.activation(alph[:, u, 0:1], gat[:, u, 2 * D:2 * D + 1], ACT.Exp, scale=-1.0).then_inc(alph_s, 1)
                act.wait_ge(ht_ready, 2 * k + 1)
                for c in range(4):
                    last = act.activation(hT[:, c], ps[:, 3, c * P:(c + 1) * P], ACT.Relu,
                                          bias=tabT[:, bass.ds(e * FC + c, 1)])
                last.then_inc(ht_act, 1)
                if not (isinstance(k, int) and k == TILES - 1):
                    hidden(k + 1)

            hidden(0)
            tiles_of(act, tile)

        @block.vector
        def _(dve):
            def norm_stats(src, f, k, s_stats):
                for t in range(TC):
                    last = dve.bn_stats(st6[:, f, t], src[:, f, t])
                last.then_inc(s_stats, 1)
                wait_apart(dve, s_stats, 2 * k - 1)
                for t in range(TC):
                    last = dve.bn_aggr(mv[:, f, t], st6[:, f, t])
                last.then_inc(s_stats, 1)

            def normalise(dst, src, f, k, s_rstd, s_out):
                dve.wait_ge(s_rstd, k)
                for t in range(TC):
                    last = dve.tensor_scalar(dst(t), src[:, f, t], mv[:, f, t, 0:1], rstd[:, f, t:t + 1],
                                             ALU.subtract, ALU.mult)
                last.then_inc(s_out, 1)

            def layer_norm(b, f, k):
                dve.wait_ge(x_got[f], 16 * b + 16)
                norm_stats(x_in, f, k, stats)
                normalise(lambda t: xn[:, f, t], x_in, f, k, rstd_s, xn_s)

            layer_norm(0, 0, 1)

            def maximum(n, s, h):
                t, c = CHUNKS[s]
                w = chunk_cols(s)
                k = 48 * n + 4 * s + h
                if t // 4 == c:
                    wait_apart(dve, s_ready, k + 1)
                else:
                    dve.wait_ge(s_ready, k + 1)
                src = ps[:, score_bank(n, s, h), 0:w]
                dst = mx[:, c + t // 4, h, t % 4:t % 4 + 1]
                if t // 4 == c:
                    dve.tensor_tensor_reduce(src, src, maskF[:, HALF - w:], 1.0, LOW,
                                             ALU.add, ALU.max, dst).then_inc(max_s, 1)
                else:
                    dve.tensor_reduce(dst, src, AX, ALU.max).then_inc(max_s, 1)

            def out_view():
                return ps[:, 7, :].rearrange("p (t h c) -> p t h c", t=TC, h=HG)

            def sum_reciprocals(n, half):
                dve.wait_ge(ot_ready, 2 * n + half + 1)
                dve.reciprocal(rec[:, :, :], out_view()[:, :, :, HD]).then_inc(rec_s, 1)

            def attention_out(n, half):
                dve.wait_ge(rec_s, 2 * n + half + 1)
                at = n * KT * 64 + half * TC * 64
                dst = ao[:, bass.ds(at, TC * 64)].rearrange("p (t h c) -> p t h c", t=TC, h=HG)
                dve.tensor_tensor(dst, out_view()[:, :, :, 0:HD], rec.unsqueeze(3).broadcast_to([P, TC, HG, HD]),
                                  ALU.mult).then_inc(ao_s, 1)

            def step_maxima(n, s, out=None):
                if s == 0:
                    after(dve, mparts_s, 2 * n - 1)
                if s == 4:
                    after(dve, mparts_s, 2 * n)
                for h in range(HG):
                    maximum(n, s, h)
                    if out is not None and h == 0:
                        sum_reciprocals(*out)
                    if out is not None and h == 1:
                        attention_out(*out)
                if s == NS - 1:
                    dve.wait_ge(max_s, 48 * n + 48)
                    dve.tensor_tensor(mx[:, 3], mx[:, 1], mx[:, 2], ALU.max).then_inc(comb_s, 1)

            def chunk(b, f, last):
                if not last:
                    layer_norm(b + f, 1 - f, 2 * b + f + 2)
                for i in range(4):
                    k = 8 * b + 4 * f + i + 1
                    p1 = parts[:, f, i, 0:HALF]
                    if last:
                        for c in range(DC):
                            maximum(0, i // 2, (2 * i + c) % HG)
                    dve.wait_ge(part1_s, k)
                    after(dve, part3_s, k - 2)
                    dve.scalar_tensor_tensor(out=resid[:, i % 2], in0=ps[:, 2 + i, :],
                                             scalar=HD ** -0.5 if i < 2 else 1.0, in1=p1,
                                             op0=ALU.mult, op1=ALU.subtract).then_inc(resid_s, 1)
                    dve.wait_ge(resid_s, k)
                    dve.tensor_copy(parts[:, f, i, HALF:2 * HALF], resid[:, i % 2]).then_inc(part2_s, 1)

            chunks_of(dve, chunk)

            for s in range(2, NS):
                step_maxima(0, s)
            dve.wait_ge(fill, 2)
            for f in range(2):
                dve.wait_ge(parts_out[f], 64 * B)

            def group(n, u, rounds=None):
                static = isinstance(n, int)
                for s in range(NS):
                    out = None
                    if s == OUT_AT[1] and not (static and n == 0):
                        out = (n - 1, 1)
                    if s == OUT_AT[0]:
                        out = (n, 0)
                    if not (static and n == NG - 1):
                        step_maxima(n + 1, s, out)
                    elif out is not None:
                        sum_reciprocals(*out)
                        attention_out(*out)

                    if static and n == NG - 1 and s == 0:
                        dve.wait_ge(st_ready, 2 * NS * (NG - 1))
                        dve.wait_ge(ao_s, 2 * G)
                        for t in range(TC):
                            last = dve.tensor_copy(stage[:, 0, t].rearrange("p (g c) -> p g c", g=G), ao_v[:, 0, t])
                        last.then_inc(stage_s, 1)
                    if static and n == NG - 1 and s == 2:
                        dve.wait_ge(at_ready, 1)
                        for c in range(DC):
                            last = dve.tensor_copy(aoT[:, 0, c], ps[:, 4 + c, :])
                        last.then_inc(at_sb, 1)

            groups_of(dve, group)
            sum_reciprocals(NG - 1, 1)
            attention_out(NG - 1, 1)

            links = [0]

            def link(ins):
                links[0] += 1
                ins.then_inc(dve_chain, 1)
                dve.wait_ge(dve_chain, links[0])

            def residual(j):
                f = j % 2
                dve.wait_ge(xr_in[f], 16 * (j // 2) + 16)
                dve.wait_ge(proj_ready, j + 1)
                if j >= 2:
                    dve.wait_ge(z_s, j - 1)
                for w in range(2):
                    dve.tensor_tensor(x1[:, f, 2 * w:2 * w + 2].rearrange("p t d -> p (t d)"), ps[:, proj_bank(j) + w, :],
                                      xr[:, f, 2 * w:2 * w + 2].rearrange("p t d -> p (t d)"),
                                      ALU.add).then_inc(x1_s, 1)
                dve.wait_ge(x1_s, 2 * j + 2)
                norm_stats(x1, f, 2 * j + 1, stats_c)

            def make_y(j):
                f = j % 2
                if j >= 2:
                    dve.wait_ge(yt_ready, j - 1)
                normalise(lambda t: ys[:, f, t], x1, f, 2 * j + 1, rstd_c, y_s)
                dve.wait_ge(y_s, j + 1)
                norm_stats(ys, f, 2 * j + 2, stats_c)

            def norm_y(j):
                f = j % 2
                if j >= 2:
                    dve.wait_ge(pk_out[f], 16 * (j // 2))
                normalise(lambda t: pks[:, f, t, 0:D], ys, f, 2 * j + 2, rstd_c, yn_s)

            def route(j):
                f = j % 2
                aff = ps[:, 6, 0:TC * E].rearrange("p (t e) -> p t e", t=TC)
                dve.wait_ge(aff_ready, j + 1)
                top = rs[:, 0]
                link(dve.tensor_reduce(top, aff, AX, ALU.max))
                dve.tensor_copy(pks[:, f, :, 2 * D], top).then_inc(score_s, 1)
                link(dve.tensor_tensor(rt[:, 0], aff, top.unsqueeze(2).broadcast_to([P, TC, E]), ALU.is_ge))
                prefer = cst[:, 0:E].unsqueeze(1).broadcast_to([P, TC, E])
                link(dve.tensor_tensor(rt[:, 1], rt[:, 0], prefer, ALU.mult))
                link(dve.tensor_reduce(rs[:, 1], rt[:, 1], AX, ALU.max))
                if j >= 2:
                    dve.wait_ge(rank_ready, j - 1)
                link(dve.tensor_tensor(ohB[:, f], rt[:, 1], rs[:, 1].unsqueeze(2).broadcast_to([P, TC, E]),
                                       ALU.is_equal))
                link(dve.tensor_reduce(csum[:, :], ohB[:, f].rearrange("p t e -> p e t"), AX, ALU.add))
                link(dve.tensor_tensor(cum[:, 1 - f], cum[:, f], csum[:, :], ALU.add))
                dve.tensor_copy(cumB[:, 1 - f], cum[:, 1 - f]).then_inc(oh_s, 1)

            def put_slots(j):
                f = j % 2
                rank = ps[:, 7, 0:TC * E].rearrange("p (t e) -> p t e", t=TC)
                first = cst[:, E:2 * E].unsqueeze(1).broadcast_to([P, TC, E])
                dve.wait_ge(rank_ready, j + 1)
                link(dve.tensor_tensor(rt[:, 2], rank, first, ALU.add))
                link(dve.tensor_tensor(rt[:, 3], rt[:, 2], ohB[:, f], ALU.mult))
                link(dve.tensor_reduce(rs[:, 2], rt[:, 3], AX, ALU.add))
                if j >= 2:
                    dve.wait_ge(ids_out[f], 16 * TC * (j // 2))
                dve.tensor_copy(slot[:, f], rs[:, 2])
                dve.tensor_copy(slot_tok[:, f], tok_id[:, j * TC:(j + 1) * TC]).then_inc(slot_s, 1)

            for j in range(CH + 1):
                if j < CH:
                    residual(j)
                if j >= 1:
                    route(j - 1)
                if j < CH:
                    make_y(j)
                if j >= 1:
                    put_slots(j - 1)
                if j < CH:
                    norm_y(j)

            dve.wait_ge(count_ready, 1)
            link(dve.tensor_copy(tt[:, 0, 0:E], ps[:, 6, 0:E]))
            grid = tcmp[:, 0:E * T].rearrange("p (e k) -> p e k", e=E)
            link(dve.tensor_tensor(grid, tt[:, 0, 0:E].unsqueeze(2).broadcast_to([P, E, T]),
                                   cst[:, 16:16 + T].unsqueeze(1).broadcast_to([P, E, T]), ALU.is_gt))
            link(dve.tensor_reduce(tt[:, 1, 0:E], grid, AX, ALU.add))
            link(dve.tensor_copy(tt[:, 2, 0:E], tt[:, 1, 0:E]))
            for e in range(1, E):
                link(dve.tensor_tensor(tt[:, 2, e:e + 1], tt[:, 2, e - 1:e], tt[:, 1, e:e + 1], ALU.add))
            past = tcmp[:, 0:TILES * (E - 1)].rearrange("p (k e) -> p k e", e=E - 1)
            ends = tt[:, 2, 0:E - 1].unsqueeze(1).broadcast_to([P, TILES, E - 1])
            number = cst[:, 48:48 + TILES].unsqueeze(2).broadcast_to([P, TILES, E - 1])
            link(dve.tensor_tensor(past, number, ends, ALU.is_ge))
            link(dve.tensor_reduce(tt[:, 3, 0:TILES], past, AX, ALU.add))
            link(dve.tensor_tensor(past, past, tt[:, 1, 0:E - 1].unsqueeze(1).broadcast_to([P, TILES, E - 1]),
                                   ALU.mult))
            link(dve.tensor_reduce(tt[:, 4, 0:TILES], past, AX, ALU.add))
            link(dve.tensor_tensor(tt[:, 5, 0:TILES], cst[:, 48:48 + TILES], tt[:, 4, 0:TILES], ALU.subtract))
            link(dve.tensor_scalar(tt[:, 6, 0:TILES], tt[:, 3, 0:TILES], float(LIST), None, ALU.mult))
            link(dve.scalar_tensor_tensor(out=tt[:, 7, 0:TILES], in0=tt[:, 5, 0:TILES], scalar=float(P),
                                          in1=tt[:, 6, 0:TILES], op0=ALU.mult, op1=ALU.add))
            dve.tensor_copy(tile_tab[:, 0, 0:TILES], tt[:, 3, 0:TILES])
            dve.tensor_copy(tile_tab[:, 1, 0:TILES], tt[:, 7, 0:TILES]).then_inc(table_s, 1)
            dve.wait_ge(table_s, 1)
            dve.memset(gat[:, :, :], 0.0).then_inc(gat_clear, 1)

            def expert_of(k):
                return dve.value_load(tile_tab[0:1, 0, bass.ds(k, 1)], min_val=0, max_val=E - 1)

            def scale_shift(k, u):
                e = expert_of(k)
                dve.wait_ge(et_ready, k + 1)
                for c in range(DC):
                    last = dve.tensor_scalar(eT[:, u, c], ps[:, 0, c * P:(c + 1) * P],
                                             tabT[:, bass.ds(e * DC + (E * FC + c), 1)],
                                             tabT[:, bass.ds(e * DC + (E * (FC + DC) + c), 1)], ALU.mult, ALU.add)
                last.then_inc(et_sb, 1)

            def hidden(k):
                dve.wait_ge(h_ready, 2 * k + 2)
                dve.tensor_copy(hs[:, HALF:], ps[:, 2, :]).then_inc(h_dve, 1)

            def tile(k, u, it):
                left = TILES - 1 - k if isinstance(k, int) else TILES
                e = expert_of(k)
                dve.wait_ge(ht_ready, 2 * k + 2)
                for c in range(4, FC):
                    last = dve.tensor_scalar(hT[:, c], ps[:, 4, (c - 4) * P:(c - 3) * P],
                                             tabT[:, bass.ds(e * FC + c, 1)], 0.0, ALU.add, ALU.max)
                last.then_inc(ht_dve, 1)
                if left >= 1:
                    hidden(k + 1)
                if left >= 2:
                    scale_shift(k + 2, (u + 2) % UNROLL)
                dve.wait_ge(alph_s, k + 1)
                dve.tensor_scalar(alph[:, u, 1:2], alph[:, u, 0:1], 1.0, None, ALU.add).then_inc(y_chain, 1)
                dve.wait_ge(y_chain, 3 * k + 1)
                dve.reciprocal(alph[:, u, 2:3], alph[:, u, 1:2]).then_inc(y_chain, 1)
                dve.wait_ge(ye_ready, k + 1)
                after(dve, out_s[u], 16 * it)
                dve.tensor_tensor(yo[:, u, 0:D], ps[:, 5 + u, 0:D], b2r[:, bass.ds(e * D, D)],
                                  ALU.add).then_inc(y_chain, 1)
                dve.wait_ge(y_chain, 3 * k + 3)
                dve.scalar_tensor_tensor(out=yo[:, u, D:2 * D], in0=yo[:, u, 0:D], scalar=alph[:, u, 2:3],
                                         in1=gat[:, u, D:2 * D], op0=ALU.mult, op1=ALU.add).then_inc(yo_s, 1)

            scale_shift(0, 0)
            hidden(0)
            scale_shift(1, 1)
            tiles_of(dve, tile)

        @block.tensor
        def _(pe):
            def transpose(dst, src, rows=P):
                return pe.transpose(dst, src, identF[0:rows, 0:rows])

            pe.wait_ge(weights_in, 16 * 8)

            def turn(k, f):
                pe.wait_ge(xn_s, k)
                for c in range(DC):
                    for t in range(TC):
                        last = transpose(ps[:, c, t * P:(t + 1) * P], xn[:, f, t, c * P:(c + 1) * P])
                    last.then_inc(xt_ready, 1)

            turn(1, 0)
            transpose(ps[:, 6, 0:TABS], tabs[0:TABS, :], TABS).then_inc(tab_ready, 1)
            pe.wait_ge(tab_sb, 1)

            def score_chunk(n, u, s, h):
                t, c = CHUNKS[s]
                k = 48 * n + 4 * s + h
                four = isinstance(n, int) and n == 0 and s > 3
                after(pe, max_s, k - 3 if four else k - 1)
                pe.matmul(ps[:, score_bank(n, s, h), 0:chunk_cols(s)],
                          q_aug[u][0:KS, t // 4, h, (t % 4) * P:(t % 4 + 1) * P],
                          k_aug[u][0:KS, h, c * HALF:c * HALF + chunk_cols(s)],
                          start=True, stop=True).then_inc(s_ready, 1)

            def chunk(b, f, last):
                k = 2 * b + f + 1
                pe.wait_ge(xt_sb, 2 * k)
                for i in range(4):
                    m = (i % 2) * P
                    after(pe, resid_s, 8 * b + 4 * f + i - 3)
                    for c in range(DC):
                        mm = pe.matmul(ps[:, 2 + i, :], wqkv[:, i // 2, c, m:m + P],
                                       xnT[:, f, c], start=(c == 0), stop=(c == DC - 1))
                        if c == DC - 1:
                            mm.then_inc(qk_ready, 1)
                        if last:
                            if i == c == 0:
                                pe.wait_ge(const_in, 16 * CONSTS)
                                pe.wait_ge(aug_in[0], 16 * AUG_DMAS)
                            score_chunk(0, 0, i // 2, (2 * i + c) % HG)
                if not last:
                    turn(k + 1, 1 - f)
                for w in range(2):
                    after(pe, v_sb, 4 * b + 2 * f + w - 1)
                    for t in range(2):
                        for c in range(DC):
                            at = (2 * w + t) * P
                            mm = pe.matmul(ps[:, 6 + w, t * D:(t + 1) * D], xnT[:, f, c, at:at + P],
                                           wqkv[:, 2, c, :], start=(c == 0), stop=(c == DC - 1))
                        if t == 1:
                            mm.then_inc(v_ready, 1)
                        if last:
                            score_chunk(0, 0, 2, 2 * w + t)

            chunks_of(pe, chunk)

            def turn_maxima(n, half):
                k = 2 * n + half
                pe.wait_ge(mparts_s, k + 1)
                after(pe, mt_sb, k)
                wait_apart(pe, ao_s, 2 * n - 1 if half else 2 * n - 2)
                pe.transpose(ps[0:48, 7, 0:P // 2].bitcast(BF16), mparts.rearrange("p a c -> p (a c)"),
                             identB[:, :]).then_inc(mt_ready, 1)

            def exp_scores(n, u, s, p):
                half, kt = STEPS[s]
                c = first_col(s)
                after(pe, exp_s, 24 * n + 2 * s + p - 1)
                for h in (2 * p, 2 * p + 1):
                    mm = pe.matmul(ps[:, h, c:], k_aug[u][0:KE, h, kt * P:(kt + 1) * P],
                                   q_aug[u][0:KE, half, h, c:], start=True, stop=s not in DIAG)
                    if s in DIAG:
                        mm = pe.matmul(ps[:, h, c:c + P], identB[:, :], laterB[:, :], start=False, stop=True)
                mm.then_inc(st_ready, 1)

            def values(n, u, s, part):
                half, kt = STEPS[s]
                c = first_col(s)
                mid = (c + HALF) // 2
                cols = slice(mid, HALF) if part else slice(c, mid)
                if part == 0:
                    if s == 0:
                        pe.wait_ge(vg_s, n + 1)
                    if s in (0, 4):
                        after(pe, o_sb_s, 2 * n + half)
                    pe.wait_ge(exp_s, 24 * n + 2 * s + 2)
                for h in range(HG):
                    mm = pe.matmul(ps[32 * h:32 * h + 32, 6, cols], v_grp[u][:, kt, h, :], probs[s % 3][:, h, cols],
                                   start=(kt == 0 and part == 0), stop=(s in (3, NS - 1) and part == 1))
                if part == 1:
                    mm.then_inc(pv_s, 1)

            def turn_output(n, half, mts):
                pe.wait_ge(o_sb_s, 2 * n + half + 1)
                after(pe, ao_s, 2 * n + half)
                pe.wait_ge(mt_sb, mts)
                for t in range(TC):
                    mm = transpose(ps[:, 7, t * P:(t + 1) * P], o_sb[:, half, t * P:(t + 1) * P])
                mm.then_inc(ot_ready, 1)

            pe.wait_ge(resid_s, 4 * CH)
            pe.wait_ge(v_sb, 2 * CH)
            for s in range(3, NS):
                for h in range(HG):
                    score_chunk(0, 0, s, h)
                if s == 6:
                    turn_maxima(0, 0)

            def turn_attention(j):
                pe.wait_ge(stage_s, j + 1)
                after(pe, at_sb, j)
                bank = 4 if j == 0 else 0
                for c in range(DC):
                    for t in range(TC):
                        mm = transpose(ps[:, bank + c, t * P:(t + 1) * P], stage[:, j % 2, t, c * P:(c + 1) * P])
                mm.then_inc(at_ready, 1)

            def project_tile(j, t):
                if t == 0:
                    pe.wait_ge(at_sb, j + 1)
                    if j >= 2:
                        pe.wait_ge(x1_s, 2 * j)
                for c in range(DC):
                    mm = pe.matmul(ps[:, proj_bank(j) + t // 2, (t % 2) * D:(t % 2 + 1) * D],
                                   aoT[:, j % 2, c, t * P:(t + 1) * P], wos[:, c, :],
                                   start=(c == 0), stop=(c == DC - 1))
                if t == TC - 1:
                    mm.then_inc(proj_ready, 1)

            def project(j):
                for t in range(TC):
                    project_tile(j, t)

            def group(n, u, rounds=None):
                static = isinstance(n, int)
                rounds = n // UNROLL + 1 if static else rounds
                nxt = (u + 1) % UNROLL
                is_last = static and n == NG - 1
                for s in range(NS):
                    if s == 0:
                        pe.wait_ge(m_in[0], 48 * n + 48)
                        if not is_last:
                            r = (n + 1) // UNROLL + 1 if static else (rounds + 1 if u == 2 else rounds)
                            pe.wait_ge(aug_in[nxt], 16 * AUG_DMAS * r)
                    if s == 4:
                        pe.wait_ge(m_in[1], 48 * n + 48)
                    behind = (n, u, s - 2) if s >= 2 else (n - 1, (u + 2) % UNROLL, NS - 2 + s)
                    has_values = s >= 2 or not (static and n == 0)
                    for i in range(HG):
                        if not is_last:
                            score_chunk(n + 1, nxt, s, i)
                        if i in (0, 3):
                            exp_scores(n, u, s, i // 2)
                        elif has_values:
                            values(*behind, i - 1)
                    if s == 0:
                        turn_maxima(n, 1)
                    if s == 4 and not (static and n == 0):
                        turn_output(n - 1, 1, 2 * n + 2)
                    if s == 6 and not is_last:
                        turn_maxima(n + 1, 0)
                    if s == 10:
                        turn_output(n, 0, 2 * n + 2 if is_last else 2 * n + 3)
                    if is_last and s == 1:
                        turn_attention(0)
                    if is_last and 4 <= s < 4 + TC:
                        project_tile(0, s - 4)

            pe.wait_ge(max_s, 4 * NS)
            groups_of(pe, group)
            for s in (NS - 2, NS - 1):
                for part in range(2):
                    values(NG - 1, 0, s, part)
            turn_output(NG - 1, 1, 2 * NG)

            def turn_y(j):
                pe.wait_ge(y_s, j + 1)
                after(pe, yt_sb, j)
                for c in range(DC):
                    for t in range(TC):
                        mm = transpose(ps[:, 4 + c, t * P:(t + 1) * P], ys[:, j % 2, t, c * P:(c + 1) * P])
                mm.then_inc(yt_ready, 1)

            cent_at = E * (FC + 2 * DC)
            centT = tabT[:, cent_at:cent_at + E * DC].rearrange("p (e c) -> p c e", c=DC)

            def affinity(j):
                pe.wait_ge(yt_sb, j + 1)
                after(pe, oh_s, j)
                for t in range(TC):
                    for c in range(DC):
                        mm = pe.matmul(ps[:, 6, t * E:(t + 1) * E],
                                       yT[:, j % 2, c, t * P:(t + 1) * P], centT[:, c, :],
                                       start=(c == 0), stop=(c == DC - 1))
                mm.then_inc(aff_ready, 1)

            def rank(j):
                f = j % 2
                pe.wait_ge(oh_s, j + 1)
                after(pe, slot_s, j)
                for t in range(TC):
                    dst = ps[:, 7, t * E:(t + 1) * E]
                    pe.matmul(dst, onesB[:, :], cumB[:, f], start=True, stop=False)
                    for q in range(t):
                        pe.matmul(dst, onesB[:, :], ohB[:, f, q], start=False, stop=False)
                    mm = pe.matmul(dst, beforeB[:, :], ohB[:, f, t], start=False, stop=True)
                mm.then_inc(rank_ready, 1)

            turn_attention(1)
            for j in range(CH):
                if j + 1 < CH:
                    project(j + 1)
                turn_y(j)
                if j >= 1:
                    rank(j - 1)
                if j + 2 < CH:
                    turn_attention(j + 2)
                affinity(j)
            rank(CH - 1)
            pe.matmul(ps[:, 6, 0:E], onesB[:, :], cumB[:, CH % 2], start=True, stop=True).then_inc(count_ready, 1)

            pe.wait_ge(table_s, 1)

            def expert_of(k):
                return pe.value_load(tile_tab[0:1, 0, bass.ds(k, 1)], min_val=0, max_val=E - 1)

            def turn_tokens(k, u, rounds):
                pe.wait_ge(gat_in[u], 16 * rounds)
                after(pe, et_sb, k)
                for c in range(DC):
                    mm = transpose(ps[:, 0, c * P:(c + 1) * P], gat[:, u, c * P:(c + 1) * P])
                mm.then_inc(et_ready, 1)

            w1_cols = w1s.rearrange("p e f -> p (e f)")
            w2_cols = w2s.rearrange("p e f -> p (e f)")

            def up(k, u):
                e = expert_of(k)
                pe.wait_ge(et_sb, k + 1)
                for half in range(2):
                    for c in range(DC):
                        mm = pe.matmul(ps[:, 1 + half, :], eT[:, u, c],
                                       w1_cols[:, bass.ds(e * (DC * F) + (c * F + half * HALF), HALF)],
                                       start=(c == 0), stop=(c == DC - 1))
                    mm.then_inc(h_ready, 1)

            def turn_hidden(k):
                for half, s in ((0, h_act), (1, h_dve)):
                    pe.wait_ge(s, k + 1)
                    for c in range(4):
                        at = half * HALF + c * P
                        mm = transpose(ps[:, 3 + half, c * P:(c + 1) * P], hs[:, at:at + P])
                    mm.then_inc(ht_ready, 1)

            def down(k, u, left, it):
                e = expert_of(k)
                for half, s in ((0, ht_act), (1, ht_dve)):
                    pe.wait_ge(s, k + 1)
                    for c in range(4 * half, 4 * half + 4):
                        mm = pe.matmul(ps[:, 5 + u, 0:D], hT[:, c], w2_cols[:, bass.ds(e * (FC * D) + c * D, D)],
                                       start=(c == 0), stop=(c == FC - 1))
                    if half == 0 and left >= 2:
                        turn_tokens(k + 2, (u + 2) % UNROLL, it + 1 if u == 0 else it + 2)
                mm.then_inc(ye_ready, 1)

            def tile(k, u, it):
                left = TILES - 1 - k if isinstance(k, int) else TILES
                turn_hidden(k)
                if left >= 1:
                    up(k + 1, (u + 1) % UNROLL)
                down(k, u, left, it)

            turn_tokens(0, 0, 1)
            pe.wait_ge(w1_in, 16 * E)
            up(0, 0)
            turn_tokens(1, 1, 1)
            pe.wait_ge(w2_in, 16 * (E + 4))
            tiles_of(pe, tile)




def shape_constants():
    import numpy as np

    bf16 = mybir.dt.np(BF16)
    eye = np.eye(P, dtype=np.float32)
    before = np.triu(np.ones((P, P), np.float32), 1).astype(bf16)
    later = np.tril(np.full((P, P), LOW, np.float32), -1).astype(bf16)
    mask = np.zeros((P, HALF), np.float32)
    mask[:, HALF - P:] = np.triu(np.full((P, P), LOW, np.float32), 1)
    slope = np.array([2.0 ** (-8.0 / H * (i + 1)) for i in range(H)], np.float32)
    rest = slope[:, None] * np.arange(L, dtype=np.float32)[None, :]
    parts = []
    for _ in range(3):
        part = rest.astype(bf16)
        parts.append(part)
        rest = rest - part.astype(np.float32)
    alibi = np.stack(parts).reshape(3, G, HG, L).transpose(1, 0, 2, 3).reshape(G * 3, HG, L)
    alibi = np.ascontiguousarray(np.tile(alibi, (B, 1, 1)))
    tokens = np.ascontiguousarray(np.arange(TOK, dtype=np.int32).reshape(T, P).T)
    row = np.zeros(96, np.float32)
    row[0:E] = E - np.arange(E)
    row[E:2 * E] = LIST * np.arange(E)
    row[16:16 + T] = P * np.arange(T)
    row[48:48 + TILES] = np.arange(TILES)
    consts = np.ascontiguousarray(np.broadcast_to(row, (P, 96)))
    return {"ident": eye, "identh": eye.astype(bf16), "before": before, "later": later, "mask": mask,
            "alibi": alibi, "ones": np.ones((3, HG * L), bf16), "tokens": tokens, "consts": consts}


_INS = ["L0_attn_x", "L0_attn_q_w", "L0_attn_k_w", "L0_attn_v_w", "L0_attn_o_w", "L0_ffn_centroids",
        "L0_ffn_ln_g", "L0_ffn_ln_b", "L0_ffn_w1", "L0_ffn_b1", "L0_ffn_w2", "L0_ffn_b2"]


def kernel(**inputs):
    import numpy as _np
    import concourse.bacc as _bacc
    from concourse import mybir as _mybir
    from concourse.bass_utils import run_bass_kernel_spmd as _run

    nc = _bacc.Bacc("TRN2", target_bir_lowering=False, num_devices=1)
    arrays, args = {}, []
    data = {name: _np.ascontiguousarray(inputs[name]) for name in _INS}
    data.update(shape_constants())
    for name, a in data.items():
        arrays[f"in_{name}_dram"] = a
        args.append(nc.dram_tensor(f"in_{name}_dram", a.shape, _mybir.dt.from_np(a.dtype), kind="ExternalInput").ap())
    args.append(nc.dram_tensor("out_0_dram", (B, L, D), _mybir.dt.float32, kind="ExternalOutput").ap())
    layer_kernel(nc, *args)
    r = _run(nc, [arrays], core_ids=[0])
    return r.results[0]["out_0_dram"]
```
